# Optimizing a Trainium2 kernel written in Bass

```python
import numpy as np
import jax
import jax.numpy as jnp

def _softmax(x, axis=-1):
    return jax.nn.softmax(x, axis=axis)

def _gelu(x):
    return jax.nn.gelu(x, approximate=True)

def _silu(x):
    return jax.nn.silu(x)

def _sigmoid(x):
    return jax.nn.sigmoid(x)

def _layernorm(x, axis=-1, eps=1e-05):
    m = jnp.mean(x, axis=axis, keepdims=True)
    v = jnp.var(x, axis=axis, keepdims=True)
    return (x - m) / jnp.sqrt(v + eps)

def _scatter_add(tgt, idx, src, axis=0):
    return tgt.at[idx].add(src)

def _segment_sum(src, seg, n):
    return jax.ops.segment_sum(src, seg, n)
kernel_name = 'mk_adj_ffn_d1_adj_r2_0ff995'

def setup_inputs(seed: int=0):
    np.random.seed(seed)
    _w = jnp.asarray

    def _rec_inputs():
        import jax
        import jax.numpy as jnp
        _gk = jax.random.key(seed)
        x = -0.0002928 + 1 * jax.random.normal(jax.random.fold_in(_gk, 1), (4096, 128), jnp.float32)
        _w = (1.0 + jnp.arange(4096, dtype=jnp.float32)) ** (-0.5)
        _w = _w / _w.mean()
        _pij = jnp.clip(0.00390625 * _w[:, None] * _w[None, :], 0.0, 1.0)
        _a = jax.random.uniform(jax.random.fold_in(_gk, 2), (4096, 4096)) < _pij
        _a = jnp.logical_or(_a, jnp.eye(4096, dtype=bool))
        _af = _a.astype(jnp.float32)
        _af = _af * jax.random.uniform(jax.random.fold_in(_gk, 3), (4096, 4096), jnp.float32, 0.05, 6.10351e-05)
        adj = _af
        return (x, adj)
    x, adj = _rec_inputs()

    def _L0_gnn_setup():
        import jax, jax.numpy as jnp
        import numpy as np
        N_NODES = 8192
        D_FEAT = 128
        key = jax.random.key(seed)
        k1, k2, k3 = jax.random.split(key, 3)
        x = jax.random.normal(k1, (N_NODES, D_FEAT), dtype=jnp.float32)
        adj_matrix = jax.random.uniform(k2, (N_NODES, N_NODES), dtype=jnp.float32) / N_NODES
        W = jax.random.normal(k3, (D_FEAT, D_FEAT), dtype=jnp.float32) / np.sqrt(D_FEAT)
        b = jnp.zeros((D_FEAT,), dtype=jnp.float32)
        return {'x': x, 'adj_matrix': adj_matrix, 'W': W, 'b': b}
    _L0_gnn_all = _L0_gnn_setup()
    _L0_gnn_in = {k: v for k, v in _L0_gnn_all.items() if k in ('W', 'b')}
    del _L0_gnn_all

    def _L0_ffn_setup():
        import jax, jax.numpy as jnp
        import numpy as np
        D_IN, D_HID, D_OUT = (128, 256, 128)
        N_EXPERTS, TOP_K = (64, 2)
        B, S = (8, 2048)
        key = jax.random.key(seed)
        ks = jax.random.split(key, 8)
        scale_in = 1.0 / np.sqrt(D_IN)
        scale_hid = 1.0 / np.sqrt(D_HID)
        return {'x': jax.random.normal(ks[0], (B, S, D_IN), dtype=jnp.float32), 'Wr': jax.random.uniform(ks[1], (D_IN, N_EXPERTS), jnp.float32, -scale_in, scale_in), 'br': jax.random.uniform(ks[2], (N_EXPERTS,), jnp.float32, -scale_in, scale_in), 'W1': jax.random.uniform(ks[3], (N_EXPERTS, D_IN, D_HID), jnp.float32, -scale_in, scale_in), 'b1': jax.random.uniform(ks[4], (N_EXPERTS, D_HID), jnp.float32, -scale_in, scale_in), 'W2': jax.random.uniform(ks[5], (N_EXPERTS, D_HID, D_OUT), jnp.float32, -scale_hid, scale_hid), 'b2': jax.random.uniform(ks[6], (N_EXPERTS, D_OUT), jnp.float32, -scale_hid, scale_hid)}
    _L0_ffn_all = _L0_ffn_setup()
    _L0_ffn_in = {k: v for k, v in _L0_ffn_all.items() if k in ('Wr', 'br', 'W1', 'b1', 'W2', 'b2')}
    del _L0_ffn_all
    return {'x': x, 'adj': adj, 'L0_gnn_W': _L0_gnn_in['W'], 'L0_gnn_b': _L0_gnn_in['b'], 'L0_ffn_Wr': _L0_ffn_in['Wr'], 'L0_ffn_br': _L0_ffn_in['br'], 'L0_ffn_W1': _L0_ffn_in['W1'], 'L0_ffn_b1': _L0_ffn_in['b1'], 'L0_ffn_W2': _L0_ffn_in['W2'], 'L0_ffn_b2': _L0_ffn_in['b2']}

def reference(x, adj, L0_gnn_W, L0_gnn_b, L0_ffn_Wr, L0_ffn_br, L0_ffn_W1, L0_ffn_b1, L0_ffn_W2, L0_ffn_b2):
    import jax
    import jax.numpy as jnp

    def _L0_gnn_ref(x, adj_matrix, W, b):
        import jax, jax.numpy as jnp
        import numpy as np
        N_NODES = 8192
        D_FEAT = 128
        h = jnp.einsum('nd,ed->ne', x, W) + b
        return jnp.matmul(adj_matrix, h)

    def _L0_ffn_ref(x, Wr, br, W1, b1, W2, b2):
        import jax, jax.numpy as jnp
        import numpy as np
        D_IN, D_HID, D_OUT = (128, 256, 128)
        N_EXPERTS, TOP_K = (64, 2)
        B, S = (8, 2048)
        Bx, Sx, D = x.shape
        xf = x.reshape(-1, D)
        T = xf.shape[0]
        E = Wr.shape[1]
        logits = xf @ Wr + br
        topk_logits, topk_idx = jax.lax.top_k(logits, TOP_K)
        gates = jax.nn.softmax(topk_logits, axis=1)
        combine = jnp.zeros((T, E), xf.dtype).at[jnp.arange(T)[:, None], topk_idx].add(gates)
        out = jnp.zeros((T, W2.shape[-1]), xf.dtype)
        for e in range(E):
            h = jax.nn.relu(xf @ W1[e] + b1[e])
            y = h @ W2[e] + b2[e]
            out = out + combine[:, e:e + 1] * y
        return out.reshape(Bx, Sx, -1)
    x = x + _L0_gnn_ref(_layernorm(x, axis=-1), adj, L0_gnn_W, L0_gnn_b)
    x = x + _L0_ffn_ref(_layernorm(x, axis=-1)[None], L0_ffn_Wr, L0_ffn_br, L0_ffn_W1, L0_ffn_b1, L0_ffn_W2, L0_ffn_b2)[0]
    return x

_drawn_inputs = setup_inputs


def setup_inputs(seed=0):
    import zlib

    import numpy as np

    out = dict(_drawn_inputs(seed))
    spreads = {'L0_gnn_b': (0.0, 0.1)}
    factors = {'L0_ffn_b1': 3.983}
    for name, (base, spread) in spreads.items():
        noise = np.random.default_rng([zlib.crc32(name.encode()), seed]).standard_normal(out[name].shape)
        drawn = base * np.exp(spread * noise) if base else spread * noise
        out[name] = jnp.asarray(drawn.astype(out[name].dtype))
    for name, factor in factors.items():
        out[name] = (out[name] * factor).astype(out[name].dtype)
    return out
```

```python
import concourse.bass as bass
from concourse import mybir
from contextlib import ExitStack

P = 128
N = 4096
D = 128
HID = 256
E = 64
K = 2
EPS = 1e-5
R_STEPS = 36
TILES = N // P
TPC = 4
CHUNK = TPC * P
CHUNKS = N // CHUNK
SLOTS = 8
CPS = TILES // SLOTS
GROUP = 8
BLOCKS = (N * K + E * (P - 1)) // P + 1
TURN = 16
QUAD = 4
QUADS = TURN // QUAD
WRING = 8
ROWS = BLOCKS * P
RW = D + 2
WCOLS = HID + HID // P * D + HID // P
C_ID, C_TRI, C_IOTA, C_DEST, C_BLK = 0, P, 2 * P, 2 * P + E, 2 * P + E + K * TILES
C_COLS = C_BLK + 1
TURNS = BLOCKS // TURN
assert BLOCKS == 128 and BLOCKS % TURN == 0


def gnn_moe(nc, x, adj_t, w_t, b, w_router, b_router, w_experts, b2, consts, out):
    F32, BF16 = mybir.dt.float32, mybir.dt.bfloat16
    I32, U32 = mybir.dt.int32, mybir.dt.uint32
    ALU, ACT, AX = mybir.AluOpType, mybir.ActivationFunctionType, mybir.AxisListType

    rows_dram = nc.dram_tensor("dispatched_rows", [ROWS, RW], F32)
    pair_out = nc.dram_tensor("pair_out", [K * N, D], F32)

    with ExitStack() as ctx:
        def sb(name, shape, dt=F32):
            return ctx.enter_context(nc.sbuf_tensor(name, shape, dt))

        def ps(name, shape=(P, 512)):
            return ctx.enter_context(nc.psum_tensor(name, list(shape), F32))

        def sem(name):
            return ctx.enter_context(nc.semaphore(name))

        cst = sb("cst", [P, C_COLS])
        ident = cst[:, C_ID:C_ID + P]
        iota_e = cst[:, C_IOTA:C_IOTA + E]
        block_start = cst[:, C_BLK:C_BLK + 1]
        tri = sb("tri", [P, P], BF16)
        ones = sb("ones", [P, P], BF16)
        eps = sb("eps", [P, 1])
        spare = sb("spare", [1, 1])
        wt = sb("wt", [P, D])
        b_bc = sb("b_bc", [P, D])
        wr = sb("wr", [P, E])
        br_bc = sb("br_bc", [P, E])
        b2_sb = sb("b2_sb", [2 * E, 2, D])
        zeros = sb("zeros", [P, 16 * RW])
        x_sb = sb("x_sb", [P, TILES, D])
        h_sb = sb("h_sb", [P, TILES, D])
        adj_sb = sb("adj_sb", [P, SLOTS, CPS, CHUNK])
        xn_t = sb("xn_t", [P, 2, P])
        h_stats = sb("h_stats", [P, TILES, 6])
        h_mv = sb("h_mv", [P, TILES, 2])
        h_rstd = sb("h_rstd", [P, TILES])
        h_sd = sb("h_sd", [P, TILES])
        agg_t = sb("agg_t", [P, CHUNK])
        stats = sb("stats", [P, TPC, 6])
        mv = sb("mv", [P, TPC, 2])
        sd = sb("sd", [P, TPC])
        rstd = sb("rstd", [P, TPC])
        xln = sb("xln", [P, TPC, D])
        xln_t = sb("xln_t", [P, CHUNK])
        logits = sb("logits", [P, TPC, E])
        top = sb("top", [P, TPC, 8])
        top_at = sb("top_at", [P, TPC, 8], U32)
        top_f = sb("top_f", [P, K, TPC])
        gap = sb("gap", [P, TPC])
        ex = sb("ex", [P, TPC])
        exp1 = sb("exp1", [P, TPC])
        gates = sb("gates", [P, K, TPC])
        onehot = sb("onehot", [P, K, TPC, E])
        chosen = sb("chosen", [P, TPC, E], BF16)
        weighted = sb("weighted", [P, K, TPC, E])
        combine = sb("combine", [P, TPC, E])
        combine_t = sb("combine_t", [P, CHUNK // 2])
        rank = sb("rank", [P, TPC, E])
        slot_a = sb("slot_a", [P, TPC, E])
        slot_b = sb("slot_b", [P, TPC, E])
        slot_c = sb("slot_c", [P, TPC, E])
        slot_k = sb("slot_k", [P, K, TPC])
        slot_of = sb("slot_of", [P, CHUNKS, K, TPC], U32)
        count = sb("count", [P, E])
        count_n = sb("count_n", [P, E])
        room = sb("room", [P, E])
        room_n = sb("room_n", [P, E])
        room_i = sb("room_i", [P, 2, E], I32)
        added = sb("added", [P, E])
        ends = sb("ends", [P, E])
        given = sb("given", [P, 1])
        shift = sb("shift", [P, E])
        shift_n = sb("shift_n", [P, E])
        shift_d = sb("shift_d", [P, E])
        opened = sb("opened", [P, E])
        zero_e = sb("zero_e", [P, E])
        le = sb("le", [P, E])
        le_n = sb("le_n", [P, 1])
        le_m = sb("le_m", [P, 1])
        expert_of = sb("expert_of", [P, 1])
        expert_row = sb("expert_row", [1, BLOCKS], I32)
        rows_sb = sb("rows_sb", [P, CHUNKS, K, TPC, RW])
        xb = sb("xb", [P, QUADS, QUAD, RW])
        wb = sb("wb", [P, WRING, WCOLS])
        xb_t = sb("xb_t", [P, 2, P])
        hid_t = sb("hid_t", [P, 2, HID // P, P])
        y_sb = sb("y_sb", [P, TURN, D])
        y_to = sb("y_to", [P, TURN], U32)
        pairs_sb = adj_sb[:, :, :, :].rearrange("p s c n -> p (s c n)")[:, 0:K * TILES * D].rearrange(
            "p (k t d) -> p k t d", k=K, d=D)

        acc = [ps(f"acc{i}") for i in range(2)]
        bank = [ps(f"bank{i}") for i in range(6)]
        agg_ps, xlnt_ps, logit_ps, rank_ps, combt_ps, bias_ps = bank

        consts_in, gnn_w_in, router_w_in = sem("consts_in"), sem("gnn_w_in"), sem("router_w_in")
        x_in = [sem(f"x_in{g}") for g in range(TILES // GROUP)]
        small_ready = sem("small_ready")
        adj_in = [sem(f"adj_in{s}") for s in range(SLOTS)]
        adj_used = sem("adj_used")
        b2_zeroed, zeros_set, rows_zeroed = sem("b2_zeroed"), sem("zeros_set"), sem("rows_zeroed")
        h_step, h_var, h_sqrt, xn_ready = sem("h_step"), sem("h_var"), sem("h_sqrt"), sem("xn_ready")
        xnt_done, xnt_copied, h_done, h_ready = sem("xnt_done"), sem("xnt_copied"), sem("h_done"), sem("h_ready")
        agg_copied, agg_back = sem("agg_copied"), sem("agg_back")
        r_step, var_ready, sd_ready = sem("r_step"), sem("var_ready"), sem("sd_ready")
        xln_ready, xlnt_done, xlnt_copied = sem("xln_ready"), sem("xlnt_done"), sem("xlnt_copied")
        logits_done, gap_ready, ex_ready = sem("logits_done"), sem("gap_ready"), sem("ex_ready")
        chosen_ready, rank_done, combine_ready = sem("chosen_ready"), sem("rank_done"), sem("combine_ready")
        combt_done, combt_copied, bias_done = sem("combt_done"), sem("combt_copied"), sem("bias_done")
        bias_added, rows_copied, slots_ready, gates_set = (
            sem("bias_added"), sem("rows_copied"), sem("slots_ready"), sem("gates_set"))
        dispatched = sem("dispatched")
        experts_turned, experts_known = sem("experts_turned"), sem("experts_known")
        xb_in = [sem(f"xb_in{s}") for s in range(QUADS)]
        xb_free = sem("xb_free")
        wb_in = [sem(f"wb_in{s}") for s in range(WRING)]
        xbt_done, xbt_copied, hid_done, hid_ready = sem("xbt_done"), sem("xbt_copied"), sem("hid_done"), sem("hid_ready")
        y_done, y_ready = sem("y_done"), sem("y_ready")
        y_out = [sem(f"y_out{s}") for s in range(TURN)]
        pairs_in = [sem(f"pairs_in{i}") for i in range(CHUNKS)]
        f_step, out_ready, stored = sem("f_step"), sem("out_ready"), sem("stored")

        block = ctx.enter_context(nc.Block())

        @block.sync
        def _(sp):
            xv = x.rearrange("(t p) d -> p t d", p=P)
            sp.dma_start(cst[:, :], consts).then_inc(consts_in, 16)
            for g in range(TILES // GROUP):
                sp.dma_start(x_sb[:, g * GROUP:(g + 1) * GROUP, :], xv[:, g * GROUP:(g + 1) * GROUP, :]).then_inc(x_in[g], 16)
                if g == 0:
                    sp.dma_start(wt[:, :], w_t).then_inc(gnn_w_in, 16)
                    sp.dma_start(b_bc[:, :], b.rearrange("(o d) -> o d", o=1).to_broadcast([P, D])).then_inc(gnn_w_in, 16)
            for s in range(SLOTS):
                sp.dma_start(adj_sb[:, s, :, :], adj_t[0, :, s * CPS:(s + 1) * CPS, :]).then_inc(adj_in[s], 16)
            sp.dma_start(wr[:, :], w_router).then_inc(router_w_in, 16)
            sp.dma_start(br_bc[:, :], b_router.rearrange("(o d) -> o d", o=1).to_broadcast([P, E])).then_inc(router_w_in, 16)
            sp.wait_ge(b2_zeroed, 1)
            for half in range(2):
                sp.dma_start(b2_sb[half * E:(half + 1) * E, half, :], b2).then_inc(router_w_in, 16)
            rows_z = rows_dram.ap().rearrange("(z p r) c -> z p (r c)", p=P, r=16)

            def load_chunk(j, zero_part):
                for s in range(SLOTS):
                    sp.wait_ge(adj_used, (j - 1) * SLOTS + s + 1)
                    sp.dma_start(adj_sb[:, s, :, :], adj_t[bass.ds(j, 1), :, s * CPS:(s + 1) * CPS, :].rearrange(
                        "o p c n -> p (o c) n")).then_inc(adj_in[s], 16)
                    if zero_part is not None and s % 2 == 1 and s < 7:
                        z = zero_part * 3 + s // 2
                        if z < rows_z.shape[0]:
                            if z == 0:
                                sp.wait_ge(zeros_set, 1)
                            sp.dma_start(rows_z[z], zeros[:, :]).then_inc(rows_zeroed, 16)

            for j in range(1, 4):
                load_chunk(j, j - 1)
            with sp.Fori(4, CHUNKS) as j:
                load_chunk(j, None)

            sp.wait_ge(experts_known, 1)
            def load_turn(i):
                for m in range(TURN):
                    n = TURN * i + m
                    if m % WRING == 0:
                        _, experts = nc.values_load_multi_w_load_instructions(
                            expert_row[0:1, bass.ds(n, WRING)], engines=[mybir.EngineType.SP], min_val=0, max_val=E - 1,
                            skip_runtime_bounds_check_because="VectorE compares them with E as it makes them")
                    if not isinstance(n, int) or n >= WRING:
                        sp.wait_ge(y_done, n - WRING + 1)
                    sp.dma_start(wb[:, m % WRING, :], w_experts[bass.ds(experts[m % WRING], 1), :, :].rearrange(
                        "o p c -> p (o c)")).then_inc(wb_in[m % WRING], 16)

            load_turn(0)
            with sp.Fori(1, TURNS) as i:
                load_turn(i)

            for m in range(TURN):
                sp.wait_ge(y_out[m], 16 * TURNS)
            pv = pair_out.ap().rearrange("(k t p) d -> p k t d", k=K, p=P)
            for c in range(CHUNKS):
                ts = slice(c * TPC, (c + 1) * TPC)
                for k in range(K):
                    sp.dma_start(pairs_sb[:, k, ts, :], pv[:, k, ts, :]).then_inc(pairs_in[c], 16)
            ov = out.rearrange("(t p) d -> p t d", p=P)
            for c in range(CHUNKS):
                ts = slice(c * TPC, (c + 1) * TPC)
                sp.wait_ge(out_ready, c + 1)
                sp.dma_start(ov[:, ts, :], x_sb[:, ts, :]).then_inc(stored, 16)
            sp.wait_ge(stored, 16 * CHUNKS)

        @block.gpsimd
        def _(pool):
            pool.memset(b2_sb[:, :, :], 0.0).then_inc(b2_zeroed, 1)
            pool.memset(zeros[:, :], 0.0).then_inc(zeros_set, 1)
            pool.wait_ge(rows_zeroed, 16 * 8)
            for j in range(CHUNKS):
                pool.wait_ge(slots_ready, j + 1)
                pool.wait_ge(gates_set, j + 1)
                pool.wait_ge(rows_copied, j + 1)
                for k in range(K):
                    for q in range(TPC):
                        pool.indirect_dma_start(
                            out=rows_dram[:, :], out_offset=bass.IndirectOffsetOnAxis(ap=slot_of[:, j, k, q:q + 1], axis=0),
                            in_=rows_sb[:, j, k, q, :], in_offset=None, bounds_check=ROWS - 1,
                            oob_is_err=False).then_inc(dispatched, 16)
            for n in range(BLOCKS):
                m = n % TURN
                pool.wait_ge(y_ready, n + 1)
                pool.indirect_dma_start(
                    out=pair_out[:, :], out_offset=bass.IndirectOffsetOnAxis(ap=y_to[:, m:m + 1], axis=0),
                    in_=y_sb[:, m, :], in_offset=None, bounds_check=K * N - 1, oob_is_err=False).then_inc(y_out[m], 16)

        @block.scalar
        def _(act):
            act.wait_ge(small_ready, 1)
            for c in range(TILES):
                if c % GROUP == 0:
                    g = c // GROUP
                    gs = slice(g * GROUP, (g + 1) * GROUP)
                    act.wait_ge(h_var, g + 1)
                    act.activation(h_sd[:, gs], h_mv[:, gs, 1], ACT.Sqrt, bias=eps[:, 0:1]).then_inc(h_sqrt, 1)
                act.wait_ge(xnt_done, c + 1)
                if c >= 2:
                    act.wait_ge(h_done, c - 1)
                act.copy(xn_t[:, c % 2, :], bank[c % 2][:, 0:P]).then_inc(xnt_copied, 1)

            def chunk(j, par):
                act.wait_ge(adj_used, SLOTS * (j + 1))
                act.copy(agg_t[:, :], acc[par][:, :]).then_inc(agg_copied, 1)
                act.wait_ge(var_ready, j + 1)
                act.activation(sd[:, :], mv[:, :, 1], ACT.Sqrt, bias=eps[:, 0:1]).then_inc(sd_ready, 1)
                act.wait_ge(xlnt_done, j + 1)
                act.copy(xln_t[:, :], xlnt_ps[:, :]).then_inc(xlnt_copied, 1)
                act.copy(rows_sb[:, bass.ds(j, 1), 0, :, 0:D], xln[:, :, :].rearrange("p (o q) d -> p o q d", o=1))
                act.copy(rows_sb[:, bass.ds(j, 1), 1, :, 0:D], xln[:, :, :].rearrange("p (o q) d -> p o q d", o=1)).then_inc(rows_copied, 1)
                act.wait_ge(gap_ready, j + 1)
                act.activation(ex[:, :], gap[:, :], ACT.Exp).then_inc(ex_ready, 1)
                act.wait_ge(combt_done, j + 1)
                act.copy(combine_t[:, :], combt_ps[:, 0:CHUNK // 2]).then_inc(combt_copied, 1)

            with act.Fori(0, CHUNKS // 2) as jj:
                for par in range(2):
                    chunk(2 * jj + par, par)

            rows_v = rows_dram.ap().rearrange("(l u p) c -> l p u c", u=QUAD, p=P)
            AHEAD = QUADS - 1

            def load_rows(load, slot):
                act.dma_start(xb[:, slot, :, :], rows_v[bass.ds(load, 1), :, :, :].rearrange(
                    "o p u c -> p (o u) c")).then_inc(xb_in[slot], 16)

            def relu_turn(i, last):
                for m in range(TURN):
                    n = TURN * i + m
                    q = m // QUAD
                    if m % QUAD == QUAD // 2 and (not last or q + AHEAD < QUADS):
                        load = QUADS * i + q + AHEAD
                        if not isinstance(load, int) or load >= QUADS:
                            act.wait_ge(xb_free, load - QUADS + 1)
                        load_rows(load, (q + AHEAD) % QUADS)
                    act.wait_ge(wb_in[m % WRING], 16 * (TURN // WRING * i + m // WRING + 1))
                    act.wait_ge(hid_done, n + 1)
                    if not isinstance(n, int) or n >= 2:
                        act.wait_ge(y_done, n - 1)
                    for f in range(HID // P):
                        last_f = act.activation(
                            hid_t[:, m % 2, f, :], bank[2 + m % 2][:, f * P:(f + 1) * P], ACT.Relu,
                            bias=wb[:, m % WRING, WCOLS - HID // P + f:WCOLS - HID // P + f + 1])
                    last_f.then_inc(hid_ready, 1)

            act.wait_ge(dispatched, 16 * CHUNKS * K * TPC)
            for load in range(AHEAD):
                load_rows(load, load)
            relu_turn(0, False)
            with act.Fori(1, TURNS - 1) as i:
                relu_turn(i, False)
            relu_turn(TURNS - 1, True)

        @block.vector
        def _(dve):
            dve.wait_ge(consts_in, 16)
            dve.tensor_copy(tri[:, :], cst[:, C_TRI:C_TRI + P])
            dve.memset(ones[:, :], 1.0)
            dve.memset(eps[:, :], EPS).then_inc(small_ready, 1)
            for t in (count, room, shift, zero_e, expert_of, given):
                last = dve.memset(t[:, :], 0.0)
            for j in range(CHUNKS):
                last = dve.tensor_copy(rows_sb[:, j, :, :, D + 1], cst[:, C_DEST:C_DEST + K * TILES].rearrange(
                    "p (k j q) -> p k j q", k=K, q=TPC)[:, :, j, :])
            last.then_inc(small_ready, 1)

            H_LAG = GROUP + 3
            steps = [0]

            def step(ins):
                steps[0] += 1
                ins.then_inc(h_step, 1)

            def settled():
                dve.wait_ge(h_step, steps[0])

            def h_tile_stats(c):
                step(dve.bn_stats(h_stats[:, c, :], x_sb[:, c, :]))

            def h_finish(c):
                dve.wait_ge(h_done, c + 1)
                dve.tensor_tensor(h_sb[:, c, :], bank[4 + c % 2][:, 0:D], b_bc[:, :], ALU.add).then_inc(h_ready, 1)

            for g in range(TILES // GROUP):
                dve.wait_ge(x_in[g], 16)
                if g == 1:
                    dve.wait_ge(gnn_w_in, 32)
                for i in range(GROUP):
                    h_tile_stats(g * GROUP + i)
                    if g * GROUP + i >= H_LAG:
                        h_finish(g * GROUP + i - H_LAG)
                settled()
                for i in range(GROUP):
                    last = dve.bn_aggr(h_mv[:, g * GROUP + i, :], h_stats[:, g * GROUP + i, :])
                last.then_inc(h_var, 1)
                dve.wait_ge(h_sqrt, g + 1)
                gs = slice(g * GROUP, (g + 1) * GROUP)
                step(dve.reciprocal(h_rstd[:, gs], h_sd[:, gs]))
                settled()
                for i in range(GROUP):
                    c = g * GROUP + i
                    dve.tensor_scalar(h_sb[:, c, :], x_sb[:, c, :], h_mv[:, c, 0:1], h_rstd[:, c:c + 1],
                                      ALU.subtract, ALU.mult).then_inc(xn_ready, 1)
            for c in range(TILES - H_LAG, TILES):
                h_finish(c)

            dve.wait_ge(router_w_in, 4 * 16)
            
            with dve.Fori(0, CHUNKS) as j:
                done = [0]

                def rstep(ins):
                    done[0] += 1
                    ins.then_inc(r_step, 1)

                def rsettled():
                    dve.wait_ge(r_step, R_STEPS * j + done[0])

                def bc(t):
                    return t[:, :].rearrange("p (o e) -> p o e", o=1).to_broadcast([P, TPC, E])

                def carry_wait():
                    dve.tensor_copy(spare[0:1, 0:1], cst[0:1, 0:1])

                x1 = x_sb[:, bass.ds(TPC * j, TPC), :]
                dve.wait_ge(agg_back, j + 1)
                rstep(dve.tensor_tensor(x1, agg_ps[:, :].rearrange("p (q d) -> p q d", d=D), x1, ALU.add))
                rsettled()
                carry_wait()
                for q in range(TPC):
                    last = dve.bn_stats(stats[:, q, :], x_sb[:, bass.ds(TPC * j + q, 1), :])
                rstep(last)
                rsettled()
                carry_wait()
                for q in range(TPC):
                    last = dve.bn_aggr(mv[:, q, :], stats[:, q, :])
                last.then_inc(var_ready, 1)
                dve.wait_ge(sd_ready, j + 1)
                rstep(dve.reciprocal(rstd[:, :], sd[:, :]))
                rsettled()
                for q in range(TPC):
                    last = dve.tensor_scalar(xln[:, q:q + 1, :], x_sb[:, bass.ds(TPC * j + q, 1), :], mv[:, q, 0:1],
                                             rstd[:, q:q + 1], ALU.subtract, ALU.mult)
                last.then_inc(xln_ready, 1)
                dve.wait_ge(logits_done, j + 1)
                rstep(dve.tensor_tensor(logits[:, :, :], logit_ps[:, 0:TPC * E].rearrange("p (q e) -> p q e", e=E),
                                        bc(br_bc), ALU.add))
                rsettled()
                carry_wait()
                for q in range(TPC):
                    last = dve.max(top[:, q, :], logits[:, q, :])
                rstep(last)
                rsettled()
                carry_wait()
                for q in range(TPC):
                    last = dve.max_index(top_at[:, q, :], top[:, q, :], logits[:, q, :])
                rstep(last)
                dve.tensor_tensor(gap[:, :], top[:, :, 1], top[:, :, 0], ALU.subtract).then_inc(gap_ready, 1)
                rsettled()
                rstep(dve.tensor_copy(top_f[:, :, :], top_at[:, :, 0:K].rearrange("p q k -> p k q")))
                rsettled()
                for k in range(K):
                    last = dve.tensor_tensor(
                        onehot[:, k, :, :], bc(iota_e),
                        top_f[:, k, :].rearrange("p (q o) -> p q o", o=1).to_broadcast([P, TPC, E]), ALU.is_equal)
                rstep(last)
                rsettled()
                dve.tensor_tensor(chosen[:, :, :], onehot[:, 0, :, :], onehot[:, 1, :, :], ALU.add).then_inc(chosen_ready, 1)
                dve.wait_ge(ex_ready, j + 1)
                rstep(dve.tensor_scalar_add(exp1[:, :], ex[:, :], 1.0))
                rsettled()
                rstep(dve.reciprocal(gates[:, 0, :], exp1[:, :]))
                rsettled()
                rstep(dve.tensor_tensor(gates[:, 1, :], ex[:, :], gates[:, 0, :], ALU.mult))
                rsettled()
                dve.tensor_copy(rows_sb[:, bass.ds(j, 1), :, :, D], gates[:, :, :].rearrange(
                    "p (o k) q -> p o k q", o=1)).then_inc(gates_set, 1)
                for k in range(K):
                    last = dve.tensor_tensor(
                        weighted[:, k, :, :], onehot[:, k, :, :],
                        gates[:, k, :].rearrange("p (q o) -> p q o", o=1).to_broadcast([P, TPC, E]), ALU.mult)
                rstep(last)
                rsettled()
                dve.tensor_tensor(combine[:, :, :], weighted[:, 0, :, :], weighted[:, 1, :, :], ALU.add).then_inc(combine_ready, 1)
                dve.wait_ge(rank_done, j + 1)
                rstep(dve.tensor_tensor(rank[:, :, :], rank_ps[:, 0:TPC * E].rearrange("p (q e) -> p q e", e=E), bc(count), ALU.add))
                rstep(dve.tensor_tensor(count_n[:, :], rank_ps[:, TPC * E:(TPC + 1) * E], count[:, :], ALU.add))
                rsettled()
                rstep(dve.tensor_copy(count[:, :], count_n[:, :]))
                rstep(dve.tensor_scalar_add(room_i[:, 0, :], count_n[:, :], float(P - 1)))
                rsettled()
                rstep(dve.tensor_scalar(room_i[:, 1, :], room_i[:, 0, :], -P, None, ALU.bitwise_and))
                rsettled()
                rstep(dve.tensor_copy(room_n[:, :], room_i[:, 1, :]))
                rstep(dve.tensor_tensor(slot_a[:, :, :], rank[:, :, :], bc(room), ALU.is_ge))
                rsettled()
                rstep(dve.tensor_tensor(added[:, :], room_n[:, :], room[:, :], ALU.subtract))
                rsettled()
                rstep(dve.tensor_tensor_scan(ends[:, :], added[:, :], zero_e[:, :], given[:, 0:1], ALU.add, ALU.add))
                rsettled()
                rstep(dve.tensor_tensor(shift_n[:, :], ends[:, :], room_n[:, :], ALU.subtract))
                rstep(dve.tensor_copy(given[:, :], ends[:, E - 1:E]))
                rstep(dve.tensor_copy(room[:, :], room_n[:, :]))
                rsettled()
                rstep(dve.tensor_tensor(shift_d[:, :], shift_n[:, :], shift[:, :], ALU.subtract))
                rsettled()
                rstep(dve.tensor_tensor(slot_b[:, :, :], slot_a[:, :, :], bc(shift_d), ALU.mult))
                rstep(dve.tensor_tensor(slot_c[:, :, :], rank[:, :, :], bc(shift), ALU.add))
                rsettled()
                rstep(dve.tensor_tensor(rank[:, :, :], slot_c[:, :, :], slot_b[:, :, :], ALU.add))
                rsettled()
                for k in range(K):
                    last = dve.tensor_tensor(weighted[:, k, :, :], onehot[:, k, :, :], rank[:, :, :], ALU.mult)
                rstep(last)
                rsettled()
                rstep(dve.reduce_sum(slot_k[:, :, :], weighted[:, :, :, :], axis=AX.X))
                rsettled()
                dve.tensor_copy(slot_of[:, bass.ds(j, 1), :, :], slot_k[:, :, :].rearrange(
                    "p (o k) q -> p o k q", o=1)).then_inc(slots_ready, 1)
                rstep(dve.scalar_tensor_tensor(opened[:, :], added[:, :], 0.0, shift_d[:, :], ALU.is_gt, ALU.mult))
                rsettled()
                rstep(dve.tensor_tensor(shift_n[:, :], opened[:, :], shift[:, :], ALU.add))
                rsettled()
                rstep(dve.tensor_copy(shift[:, :], shift_n[:, :]))
                rstep(dve.tensor_scalar(le[:, :], ends[:, :], block_start, 0.0, ALU.is_le, ALU.add, accum_out=le_n[:, :]))
                rsettled()
                rstep(dve.scalar_tensor_tensor(le_m[:, :], le_n[:, :], float(E), le_n[:, :], ALU.is_lt, ALU.mult))
                rsettled()
                rstep(dve.tensor_tensor(expert_of[:, :], expert_of[:, :], le_m[:, :], ALU.add))
                dve.wait_ge(bias_done, j + 1)
                dve.tensor_tensor(x1, bias_ps[:, :].rearrange("p (q d) -> p q d", d=D), x1, ALU.add).then_inc(bias_added, 1)
                rsettled()
                assert done[0] == R_STEPS, done[0]
            dve.wait_ge(r_step, R_STEPS * CHUNKS)
            dve.wait_ge(experts_turned, 1)
            dve.tensor_copy(expert_row[0:1, :], logit_ps[0:1, 0:BLOCKS]).then_inc(experts_known, 1)

            def copy_t(n, m):
                dve.wait_ge(xbt_done, n + 1)
                if not isinstance(n, int) or n >= 2:
                    dve.wait_ge(hid_done, n - 1)
                dve.tensor_copy(xb_t[:, m % 2, :], bank[m % 2][:, 0:P]).then_inc(xbt_copied, 1)

            def scale_turn(i, first, last):
                for m in range(TURN):
                    n = TURN * i + m
                    if not last or m + 2 < TURN:
                        copy_t(n + 2, m)
                    if m % QUAD == 0:
                        dve.wait_ge(xb_in[m // QUAD], 16 * (i + 1))
                        if not first:
                            for u in range(QUAD):
                                dve.wait_ge(y_out[m + u], 16 * i)
                        dve.tensor_scalar(y_to[:, m:m + QUAD], xb[:, m // QUAD, :, D + 1], -1.0, float(K * N), ALU.mult, ALU.add)
                    dve.wait_ge(y_done, n + 1)
                    dve.tensor_scalar(y_sb[:, m, :], bank[4 + m % 2][:, 0:D], xb[:, m // QUAD, m % QUAD, D:D + 1], None,
                                      ALU.mult).then_inc(y_ready, 1)
                    if m % QUAD == QUAD - 1:
                        dve.engine_nop().then_inc(xb_free, 1)

            copy_t(0, 0)
            copy_t(1, 1)
            scale_turn(0, True, False)
            with dve.Fori(1, TURNS - 1) as i:
                scale_turn(i, False, False)
            scale_turn(TURNS - 1, False, True)

            for c in range(CHUNKS):
                ts = slice(c * TPC, (c + 1) * TPC)
                dve.wait_ge(pairs_in[c], 16 * K)
                dve.tensor_tensor(x_sb[:, ts, :], x_sb[:, ts, :], pairs_sb[:, 0, ts, :], ALU.add).then_inc(f_step, 1)
                dve.wait_ge(f_step, c + 1)
                dve.tensor_tensor(x_sb[:, ts, :], x_sb[:, ts, :], pairs_sb[:, 1, ts, :], ALU.add).then_inc(out_ready, 1)

        @block.tensor
        def _(pe):
            def accumulate(s, bank_acc):
                for i in range(CPS):
                    c = s * CPS + i
                    last = pe.matmul(bank_acc[:, :], h_sb[:, c, :], adj_sb[:, s, i, :], start=(c == 0), stop=(c == TILES - 1))
                last.then_inc(adj_used, 1)

            pe.wait_ge(consts_in, 16)
            for c in range(TILES + 5):
                if c == 0:
                    pe.wait_ge(gnn_w_in, 32)
                if 2 <= c < TILES + 2:
                    t = c - 2
                    pe.wait_ge(xnt_copied, t + 1)
                    if t >= 2:
                        pe.wait_ge(h_ready, t - 1)
                    pe.matmul(bank[4 + t % 2][:, 0:D], xn_t[:, t % 2, :], wt[:, :], start=True, stop=True).then_inc(h_done, 1)
                if c >= 5:
                    t = c - 5
                    pe.wait_ge(h_ready, t + 1)
                    if t % CPS == 0:
                        pe.wait_ge(adj_in[t // CPS], 16)
                    last = pe.matmul(acc[0][:, :], h_sb[:, t, :], adj_sb[:, t // CPS, t % CPS, :], start=(t == 0), stop=(t == TILES - 1))
                    if t % CPS == CPS - 1:
                        last.then_inc(adj_used, 1)
                if c < TILES:
                    pe.wait_ge(xn_ready, c + 1)
                    pe.transpose(bank[c % 2][:, 0:P], h_sb[:, c, :], ident).then_inc(xnt_done, 1)

            def back(j):
                pe.wait_ge(agg_copied, j + 1)
                for q in range(TPC):
                    last = pe.transpose(agg_ps[:, q * P:(q + 1) * P], agg_t[:, q * P:(q + 1) * P], ident)
                last.then_inc(agg_back, 1)

            def turn_rows(j):
                pe.wait_ge(xln_ready, j + 1)
                for q in range(TPC):
                    last = pe.transpose(xlnt_ps[:, q * P:(q + 1) * P], xln[:, q, :], ident)
                last.then_inc(xlnt_done, 1)

            def route(j):
                pe.wait_ge(xlnt_copied, j + 1)
                for q in range(TPC):
                    last = pe.matmul(logit_ps[:, q * E:(q + 1) * E], xln_t[:, q * P:(q + 1) * P], wr[:, :], start=True, stop=True)
                last.then_inc(logits_done, 1)

            def count_ranks(j):
                pe.wait_ge(chosen_ready, j + 1)
                for q in range(TPC + 1):
                    for r in range(min(q + 1, TPC)):
                        last = pe.matmul(rank_ps[:, q * E:(q + 1) * E], (tri if r == q else ones)[:, :], chosen[:, r, :],
                                         start=(r == 0), stop=(r == min(q, TPC - 1)))
                last.then_inc(rank_done, 1)

            def turn_combine(j):
                pe.wait_ge(combine_ready, j + 1)
                for h in range(TPC // 2):
                    last = pe.transpose(combt_ps[:, h * P:(h + 1) * P], combine[:, 2 * h:2 * h + 2, :].rearrange(
                        "p q e -> p (q e)"), ident)
                last.then_inc(combt_done, 1)

            def second_bias(j):
                pe.wait_ge(combt_copied, j + 1)
                for h in range(TPC // 2):
                    last = pe.matmul(bias_ps[:, 2 * h * D:2 * (h + 1) * D], combine_t[:, h * P:(h + 1) * P],
                                     b2_sb[:, :, :].rearrange("p h d -> p (h d)"), start=True, stop=True)
                last.then_inc(bias_done, 1)

            pieces = {0: back, 2: turn_rows, 3: route, 5: count_ranks, 6: turn_combine, 7: second_bias}

            def chunk(j, par):
                for s in range(SLOTS):
                    pe.wait_ge(adj_in[s], 16 * (j + 1))
                    accumulate(s, acc[par])
                    if s in pieces:
                        pieces[s](j - 1)

            pe.wait_ge(router_w_in, 4 * 16)
            pe.wait_ge(small_ready, 2)
            with pe.Fori(0, (CHUNKS - 2) // 2) as jj:
                chunk(2 * jj + 1, 1)
                chunk(2 * jj + 2, 0)
            chunk(CHUNKS - 1, 1)
            for s in sorted(pieces):
                pieces[s](CHUNKS - 1)
            pe.wait_ge(r_step, R_STEPS * CHUNKS)
            pe.matmul(logit_ps[0:1, 0:BLOCKS], expert_of[:, 0:1], ident, start=True, stop=True).then_inc(experts_turned, 1)

            def turn_block(i, m):
                n = TURN * i + m
                if m % QUAD == 0:
                    pe.wait_ge(xb_in[m // QUAD], 16 * (i + 1))
                pe.transpose(bank[m % 2][:, 0:P], xb[:, m // QUAD, m % QUAD, 0:D], ident).then_inc(xbt_done, 1)

            def first_layer(i, m):
                n = TURN * i + m
                pe.wait_ge(wb_in[m % WRING], 16 * (TURN // WRING * i + m // WRING + 1))
                pe.wait_ge(xbt_copied, n + 1)
                for f in range(HID // P):
                    last = pe.matmul(bank[2 + m % 2][:, f * P:(f + 1) * P], wb[:, m % WRING, f * P:(f + 1) * P], xb_t[:, m % 2, :],
                                     start=True, stop=True)
                last.then_inc(hid_done, 1)

            def second_layer(i, m):
                n = TURN * i + m
                pe.wait_ge(hid_ready, n + 1)
                if not isinstance(n, int) or n >= 2:
                    pe.wait_ge(y_ready, n - 1)
                for f in range(HID // P):
                    last = pe.matmul(bank[4 + m % 2][:, 0:D], hid_t[:, m % 2, f, :], wb[:, m % WRING, HID + f * D:HID + (f + 1) * D],
                                     start=(f == 0), stop=(f == HID // P - 1))
                last.then_inc(y_done, 1)

            def expert_turn(i, last):
                for m in range(TURN):
                    if not last or m + 2 < TURN:
                        turn_block(i + (m + 2) // TURN, (m + 2) % TURN)
                    if not last or m + 1 < TURN:
                        first_layer(i + (m + 1) // TURN, (m + 1) % TURN)
                    second_layer(i, m)

            pe.wait_ge(experts_known, 1)
            turn_block(0, 0)
            turn_block(0, 1)
            first_layer(0, 0)
            expert_turn(0, False)
            with pe.Fori(1, TURNS - 1) as i:
                expert_turn(i, False)
            expert_turn(TURNS - 1, True)


def kernel(x, adj, L0_gnn_W, L0_gnn_b, L0_ffn_Wr, L0_ffn_br, L0_ffn_W1, L0_ffn_b1, L0_ffn_W2, L0_ffn_b2):
    import numpy as np
    import concourse.bacc as bacc
    from concourse.bass_utils import run_bass_kernel_spmd

    adj_t = np.asarray(adj).reshape(CHUNKS, CHUNK, TILES, P).transpose(0, 3, 2, 1)
    w1 = np.asarray(L0_ffn_W1)
    w2 = np.asarray(L0_ffn_W2).reshape(E, HID // P, P, D).transpose(0, 2, 1, 3).reshape(E, P, HID // P * D)
    b1 = np.asarray(L0_ffn_b1).reshape(E, HID // P, P).transpose(0, 2, 1)
    consts = np.zeros((P, C_COLS), np.float32)
    consts[:, C_ID:C_ID + P] = np.eye(P)
    consts[:, C_TRI:C_TRI + P] = np.triu(np.ones((P, P)), 1)
    consts[:, C_IOTA:C_IOTA + E] = np.arange(E)
    consts[:, C_DEST:C_BLK] = K * N - (np.arange(K * TILES)[None, :] * P + np.arange(P)[:, None])
    consts[:, C_BLK] = np.arange(P) * P
    ins = {
        "x": x, "adj_t": adj_t, "w_t": np.asarray(L0_gnn_W).T, "b": L0_gnn_b, "w_router": L0_ffn_Wr,
        "b_router": L0_ffn_br, "w_experts": np.concatenate([w1, w2, b1], axis=2), "b2": L0_ffn_b2, "consts": consts,
    }
    ins = {name: np.ascontiguousarray(a) for name, a in ins.items()}
    nc = bacc.Bacc("TRN2", target_bir_lowering=False, num_devices=1)
    F32 = mybir.dt.float32
    args = {name: nc.dram_tensor(name, a.shape, F32, kind="ExternalInput").ap() for name, a in ins.items()}
    out = nc.dram_tensor("out", [N, D], F32, kind="ExternalOutput").ap()
    gnn_moe(nc, **args, out=out)
    r = run_bass_kernel_spmd(nc, [ins], core_ids=[0])
    return r.results[0]["out"]
```

```python
import concourse.bass as bass
from concourse import mybir
from contextlib import ExitStack

P = 128
N = 4096
D = 128
HID = 256
E = 64
K = 2
EPS = 1e-5
R_STEPS = 37
TILES = N // P
TPC = 4
CHUNK = TPC * P
WHOLE = TILES // TPC - 1
TAIL = TPC // 2
CHUNKS = WHOLE + 2
SLOTS = 8
CPS = TILES // SLOTS
OUTS = TILES // TPC
GROUP = 4
BLOCKS = (N * K + E * (P - 1)) // P + 1
TURN = 16
QUAD = 4
QUADS = TURN // QUAD
WRING = TURN
LOOKUP = 8
ROWS = BLOCKS * P
RW = D + 2
WCOLS = HID + HID // P * D + HID // P
C_ID, C_TRI, C_IOTA, C_DEST, C_BLK = 0, P, 2 * P, 2 * P + E, 2 * P + E + K * TILES
C_COLS = C_BLK + 1
TURNS = BLOCKS // TURN
DONE_AT = [(c + 1) * K * CHUNK // P + E for c in range(OUTS)]
assert DONE_AT[-1] == BLOCKS
BIAS_AT = (1, 4, 5, 9, 11)
LOAD_AFTER = {n + WRING + 3: c for c, n in enumerate(DONE_AT) if n + WRING + 3 < BLOCKS}
SUM_AFTER = {n + 28: c for c, n in enumerate(DONE_AT) if n + 28 < BLOCKS}
STORE_AFTER = {n + 48: c for c, n in enumerate(DONE_AT) if n + 48 < BLOCKS}
PLAIN = min(LOAD_AFTER) // TURN
assert BLOCKS == 128 and BLOCKS % TURN == 0 and TURNS == OUTS


def gnn_moe(nc, x, adj_t, adj_tail, w_t, b, w_router, b_router, w_experts, b2, consts, out):
    F32, BF16 = mybir.dt.float32, mybir.dt.bfloat16
    I32, U32 = mybir.dt.int32, mybir.dt.uint32
    ALU, ACT, AX = mybir.AluOpType, mybir.ActivationFunctionType, mybir.AxisListType

    rows_dram = nc.dram_tensor("dispatched_rows", [ROWS, RW], F32)
    pair_out = nc.dram_tensor("pair_out", [K * N, D], F32)

    with ExitStack() as ctx:
        def sb(name, shape, dt=F32):
            return ctx.enter_context(nc.sbuf_tensor(name, shape, dt))

        def ps(name, shape=(P, 512)):
            return ctx.enter_context(nc.psum_tensor(name, list(shape), F32))

        def sem(name):
            return ctx.enter_context(nc.semaphore(name))

        cst = sb("cst", [P, C_COLS])
        ident = cst[:, C_ID:C_ID + P]
        iota_e = cst[:, C_IOTA:C_IOTA + E]
        block_start = cst[:, C_BLK:C_BLK + 1]
        tri = sb("tri", [P, P], BF16)
        ones = sb("ones", [P, P], BF16)
        eps = sb("eps", [P, 1])
        spare = sb("spare", [1, 1])
        wt = sb("wt", [P, D])
        b_bc = sb("b_bc", [P, D])
        wr = sb("wr", [P, E])
        br_bc = sb("br_bc", [P, E])
        b2_sb = sb("b2_sb", [2 * E, 2, D])
        zeros = sb("zeros", [P, 16 * RW])
        x_sb = sb("x_sb", [P, TILES, D])
        h_sb = sb("h_sb", [P, TILES, D])
        adj_sb = sb("adj_sb", [P, SLOTS, CPS, CHUNK])
        xn_t = sb("xn_t", [P, 2, P])
        h_stats = sb("h_stats", [P, TILES, 6])
        h_mv = sb("h_mv", [P, TILES, 2])
        h_rstd = sb("h_rstd", [P, TILES])
        h_sd = sb("h_sd", [P, TILES])
        agg_t = sb("agg_t", [P, CHUNK])
        stats = sb("stats", [P, TPC, 6])
        mv = sb("mv", [P, TPC, 2])
        sd = sb("sd", [P, TPC])
        rstd = sb("rstd", [P, TPC])
        xln = sb("xln", [P, TPC, D])
        xln_t = sb("xln_t", [P, CHUNK])
        logits = sb("logits", [P, TPC, E])
        top = sb("top", [P, TPC, 8])
        top_at = sb("top_at", [P, TPC, 8], U32)
        top_f = sb("top_f", [P, K, TPC])
        gap = sb("gap", [P, TPC])
        ex = sb("ex", [P, TPC])
        exp1 = sb("exp1", [P, TPC])
        gates = sb("gates", [P, K, TPC])
        onehot = sb("onehot", [P, K, TPC, E])
        chosen = sb("chosen", [P, TPC, E], BF16)
        weighted = sb("weighted", [P, K, TPC, E])
        combine = sb("combine", [P, TILES, E])
        staged = sb("staged", [P, TPC, E])
        combine_t = sb("combine_t", [P, CHUNK // 2])
        slot = sb("slot", [P, TPC, E])
        slot_a = sb("slot_a", [P, TPC, E])
        slot_b = sb("slot_b", [P, TPC, E])
        slot_c = sb("slot_c", [P, TPC, E])
        slot_k = sb("slot_k", [P, K, TPC])
        slot_of = sb("slot_of", [P, K, TILES], U32)
        count = sb("count", [P, E])
        count_n = sb("count_n", [P, E])
        room = sb("room", [P, E])
        room_n = sb("room_n", [P, E])
        room_i = sb("room_i", [P, 2, E], I32)
        added = sb("added", [P, E])
        ends = sb("ends", [P, E])
        given = sb("given", [P, 1])
        shift = sb("shift", [P, E])
        shift_n = sb("shift_n", [P, E])
        shift_d = sb("shift_d", [P, E])
        left = sb("left", [P, E])
        base = sb("base", [P, E])
        opened = sb("opened", [P, E])
        zero_e = sb("zero_e", [P, E])
        le = sb("le", [P, E])
        le_n = sb("le_n", [P, 1])
        le_m = sb("le_m", [P, 1])
        expert_of = sb("expert_of", [P, 1])
        expert_row = sb("expert_row", [1, BLOCKS], I32)
        rows_sb = sb("rows_sb", [P, K, TILES, RW])
        xb = sb("xb", [P, QUADS, QUAD, RW])
        wb = sb("wb", [P, WRING // 2, WCOLS])
        xb_t = sb("xb_t", [P, 2, P])
        hid_t = sb("hid_t", [P, 2, HID // P, P])
        y_sb = h_sb
        y_to = sb("y_to", [P, TURN], U32)
        adj_flat = adj_sb[:, :, :, :].rearrange("p s c n -> p (s c n)")
        adj_half = SLOTS // 2 * CPS * CHUNK
        pairs_sb = adj_flat[:, adj_half:adj_half + K * TILES * D].rearrange("p (k t d) -> p k t d", k=K, d=D)
        wb_more = adj_flat[:, 0:WRING // 2 * WCOLS].rearrange("p (s w) -> p s w", w=WCOLS)

        def weights(m, a, b):
            return wb[:, m, a:b] if m < WRING // 2 else wb_more[:, m - WRING // 2, a:b]

        tail_sb = adj_sb[:, :, :, :].rearrange("p s c n -> p s (c n)").rearrange("p s (c n) -> p s c n", n=TAIL * P)

        acc = [ps(f"acc{i}") for i in range(2)]
        bank = [ps(f"bank{i}") for i in range(6)]
        agg_ps, xlnt_ps, logit_ps, rank_ps, expert_ps = bank[0:5]
        combt_ps, bias_ps = acc

        consts_in, gnn_w_in, router_w_in = sem("consts_in"), sem("gnn_w_in"), sem("router_w_in")
        x_in = [sem(f"x_in{g}") for g in range(TILES // GROUP)]
        small_ready = sem("small_ready")
        adj_in = [sem(f"adj_in{s}") for s in range(SLOTS)]
        adj_used = sem("adj_used")
        b2_zeroed, zeros_set, rows_zeroed = sem("b2_zeroed"), sem("zeros_set"), sem("rows_zeroed")
        h_step, h_var, h_sqrt, xn_ready = sem("h_step"), sem("h_var"), sem("h_sqrt"), sem("xn_ready")
        xnt_done, xnt_copied, h_done, h_ready = sem("xnt_done"), sem("xnt_copied"), sem("h_done"), sem("h_ready")
        agg_copied, agg_back = sem("agg_copied"), sem("agg_back")
        r_step, var_ready, sd_ready = sem("r_step"), sem("var_ready"), sem("sd_ready")
        xln_ready, xlnt_done, xlnt_copied = sem("xln_ready"), sem("xlnt_done"), sem("xlnt_copied")
        logits_done, gap_ready, ex_ready = sem("logits_done"), sem("gap_ready"), sem("ex_ready")
        chosen_ready, rank_done, combine_ready = sem("chosen_ready"), sem("rank_done"), sem("combine_ready")
        combt_done, combt_copied, bias_done = sem("combt_done"), sem("combt_copied"), sem("bias_done")
        gates_staged = sem("gates_staged")
        bias_added, rows_copied, slots_ready, gates_set = (
            sem("bias_added"), sem("rows_copied"), sem("slots_ready"), sem("gates_set"))
        dispatched = sem("dispatched")
        experts_turned, experts_known = sem("experts_turned"), sem("experts_known")
        xb_in = [sem(f"xb_in{s}") for s in range(QUADS)]
        xb_free = sem("xb_free")
        wb_in = [sem(f"wb_in{s}") for s in range(WRING)]
        xbt_done, xbt_copied, hid_done, hid_ready = sem("xbt_done"), sem("xbt_copied"), sem("hid_done"), sem("hid_ready")
        y_done, y_ready = sem("y_done"), sem("y_ready")
        y_out = [sem(f"y_out{s}") for s in range(TURN)]
        pairs_in = [sem(f"pairs_in{i}") for i in range(OUTS)]
        f_step, out_ready, stored = sem("f_step"), sem("out_ready"), sem("stored")

        block = ctx.enter_context(nc.Block())

        @block.sync
        def _(sp):
            xv = x.rearrange("(t p) d -> p t d", p=P)
            for g in range(TILES // GROUP):
                sp.dma_start(x_sb[:, g * GROUP:(g + 1) * GROUP, :], xv[:, g * GROUP:(g + 1) * GROUP, :]).then_inc(x_in[g], 16)
                if g == 0:
                    sp.dma_start(cst[:, :], consts).then_inc(consts_in, 16)
                if g == 1:
                    sp.dma_start(wt[:, :], w_t).then_inc(gnn_w_in, 16)
                    sp.dma_start(b_bc[:, :], b.rearrange("(o d) -> o d", o=1).to_broadcast([P, D])).then_inc(gnn_w_in, 16)
            for s in range(SLOTS):
                sp.dma_start(adj_sb[:, s, :, :], adj_t[0, :, s * CPS:(s + 1) * CPS, :]).then_inc(adj_in[s], 16)
            sp.dma_start(wr[:, :], w_router).then_inc(router_w_in, 16)
            sp.dma_start(br_bc[:, :], b_router.rearrange("(o d) -> o d", o=1).to_broadcast([P, E])).then_inc(router_w_in, 16)
            sp.wait_ge(b2_zeroed, 1)
            for half in range(2):
                sp.dma_start(b2_sb[half * E:(half + 1) * E, half, :], b2).then_inc(router_w_in, 16)
            rows_z = rows_dram.ap().rearrange("(z p r) c -> z p (r c)", p=P, r=16)

            def load_chunk(j, zero_part):
                for s in range(SLOTS):
                    sp.wait_ge(adj_used, (j - 1) * SLOTS + s + 1)
                    sp.dma_start(adj_sb[:, s, :, :], adj_t[bass.ds(j, 1), :, s * CPS:(s + 1) * CPS, :].rearrange(
                        "o p c n -> p (o c) n")).then_inc(adj_in[s], 16)
                    if zero_part is not None and s % 2 == 1 and s < 7:
                        z = zero_part * 3 + s // 2
                        if z < rows_z.shape[0]:
                            if z == 0:
                                sp.wait_ge(zeros_set, 1)
                            sp.dma_start(rows_z[z], zeros[:, :]).then_inc(rows_zeroed, 16)

            for j in range(1, 4):
                load_chunk(j, j - 1)
            with sp.Fori(4, WHOLE) as j:
                load_chunk(j, None)
            for c in range(2):
                for h in range(SLOTS // 2):
                    s = c * SLOTS // 2 + h
                    sp.wait_ge(adj_used, (WHOLE - 1) * SLOTS + s + 1)
                    sp.dma_start(tail_sb[:, s, :, :], adj_tail[c, :, h * 2 * CPS:(h + 1) * 2 * CPS, :]).then_inc(adj_in[s], 16)

            pv = pair_out.ap().rearrange("(k t p) d -> p k t d", k=K, p=P)
            ov = out.rearrange("(t p) d -> p t d", p=P)

            def load_pairs(c):
                for m in range(TURN):
                    sp.wait_ge(y_out[m], 16 * (DONE_AT[c] // TURN + (m < DONE_AT[c] % TURN)))
                ts = slice(c * TPC, (c + 1) * TPC)
                for k in range(K):
                    sp.dma_start(pairs_sb[:, k, ts, :], pv[:, k, ts, :]).then_inc(pairs_in[c], 16)

            def store(c):
                ts = slice(c * TPC, (c + 1) * TPC)
                sp.wait_ge(out_ready, c + 1)
                sp.dma_start(ov[:, ts, :], x_sb[:, ts, :]).then_inc(stored, 16)

            def load_turn(i):
                for m in range(TURN):
                    n = TURN * i + m
                    if m % LOOKUP == 0:
                        _, experts = nc.values_load_multi_w_load_instructions(
                            expert_row[0:1, bass.ds(n, LOOKUP)], engines=[mybir.EngineType.SP], min_val=0, max_val=E - 1,
                            skip_runtime_bounds_check_because="VectorE compares them with E as it makes them")
                    if not isinstance(n, int) or n >= WRING:
                        sp.wait_ge(y_done, n - WRING + 1)
                    sp.dma_start(weights(m, 0, WCOLS), w_experts[bass.ds(experts[m % LOOKUP], 1), :, :].rearrange(
                        "o p c -> p (o c)")).then_inc(wb_in[m], 16)
                    if isinstance(n, int) and n in LOAD_AFTER:
                        load_pairs(LOAD_AFTER[n])
                    if isinstance(n, int) and n in STORE_AFTER:
                        store(STORE_AFTER[n])

            sp.wait_ge(experts_known, 1)
            sp.wait_ge(adj_used, SLOTS * WHOLE + SLOTS // 2)
            load_turn(0)
            sp.wait_ge(experts_known, 2)
            with sp.Fori(1, PLAIN) as i:
                load_turn(i)
            for i in range(PLAIN, TURNS):
                load_turn(i)
            for c in range(len(LOAD_AFTER), OUTS):
                load_pairs(c)
            for c in range(len(STORE_AFTER), OUTS):
                store(c)
            sp.wait_ge(stored, 16 * OUTS)

        @block.gpsimd
        def _(pool):
            pool.memset(b2_sb[:, :, :], 0.0).then_inc(b2_zeroed, 1)
            pool.memset(zeros[:, :], 0.0).then_inc(zeros_set, 1)
            pool.wait_ge(rows_zeroed, 16 * 8)
            for j in range(CHUNKS):
                pool.wait_ge(slots_ready, j + 1)
                pool.wait_ge(gates_set, j + 1)
                pool.wait_ge(rows_copied, j + 1)
                first, tiles = (j * TPC, TPC) if j < WHOLE else (WHOLE * TPC + (j - WHOLE) * TAIL, TAIL)
                for t in range(first, first + tiles):
                    for k in range(K):
                        pool.indirect_dma_start(
                            out=rows_dram[:, :], out_offset=bass.IndirectOffsetOnAxis(ap=slot_of[:, k, t:t + 1], axis=0),
                            in_=rows_sb[:, k, t, :], in_offset=None, bounds_check=ROWS - 1,
                            oob_is_err=False).then_inc(dispatched, 16)
            for n in range(BLOCKS):
                m = n % TURN
                pool.wait_ge(y_ready, n + 1)
                pool.indirect_dma_start(
                    out=pair_out[:, :], out_offset=bass.IndirectOffsetOnAxis(ap=y_to[:, m:m + 1], axis=0),
                    in_=y_sb[:, m, :], in_offset=None, bounds_check=K * N - 1, oob_is_err=False).then_inc(y_out[m], 16)

        @block.scalar
        def _(act):
            act.wait_ge(small_ready, 1)
            for c in range(TILES):
                if c % GROUP == 0:
                    g = c // GROUP
                    gs = slice(g * GROUP, (g + 1) * GROUP)
                    act.wait_ge(h_var, g + 1)
                    act.activation(h_sd[:, gs], h_mv[:, gs, 1], ACT.Sqrt, bias=eps[:, 0:1]).then_inc(h_sqrt, 1)
                act.wait_ge(xnt_done, c + 1)
                if c >= 2:
                    act.wait_ge(h_done, c - 1)
                act.copy(xn_t[:, c % 2, :], bank[c % 2][:, 0:P]).then_inc(xnt_copied, 1)

            def chunk(j, par, first, tiles):
                used = SLOTS * (j + 1) if tiles == TPC else SLOTS * WHOLE + SLOTS // 2 * (j - WHOLE + 1)
                act.wait_ge(adj_used, used)
                act.copy(agg_t[:, 0:tiles * P], acc[par][:, 0:tiles * P]).then_inc(agg_copied, 1)
                act.wait_ge(var_ready, j + 1)
                act.activation(sd[:, 0:tiles], mv[:, 0:tiles, 1], ACT.Sqrt, bias=eps[:, 0:1]).then_inc(sd_ready, 1)
                act.wait_ge(xlnt_done, j + 1)
                act.copy(xln_t[:, 0:tiles * P], xlnt_ps[:, 0:tiles * P]).then_inc(xlnt_copied, 1)
                for k in range(K):
                    last = act.copy(rows_sb[:, k, bass.ds(first, tiles), 0:D], xln[:, 0:tiles, :])
                last.then_inc(rows_copied, 1)
                act.wait_ge(gap_ready, j + 1)
                act.activation(ex[:, 0:tiles], gap[:, 0:tiles], ACT.Exp).then_inc(ex_ready, 1)

            with act.Fori(0, (WHOLE - 1) // 2) as jj:
                for par in range(2):
                    chunk(2 * jj + par, par, TPC * (2 * jj + par), TPC)
            chunk(WHOLE - 1, (WHOLE - 1) % 2, TPC * (WHOLE - 1), TPC)
            for c in range(2):
                chunk(WHOLE + c, (WHOLE + c) % 2, TPC * WHOLE + TAIL * c, TAIL)

            rows_v = rows_dram.ap().rearrange("(l u p) c -> l p u c", u=QUAD, p=P)
            AHEAD = QUADS - 1

            def load_rows(load, slot):
                act.dma_start(xb[:, slot, :, :], rows_v[bass.ds(load, 1), :, :, :].rearrange(
                    "o p u c -> p (o u) c")).then_inc(xb_in[slot], 16)

            def relu_turn(i, last):
                for m in range(TURN):
                    n = TURN * i + m
                    q = m // QUAD
                    if m % QUAD == QUAD // 2 and (not last or q + AHEAD < QUADS):
                        load = QUADS * i + q + AHEAD
                        if not isinstance(load, int) or load >= QUADS:
                            act.wait_ge(xb_free, load - QUADS + 1)
                        load_rows(load, (q + AHEAD) % QUADS)
                    act.wait_ge(wb_in[m], 16 * (i + 1))
                    act.wait_ge(hid_done, n + 1)
                    if not isinstance(n, int) or n >= 2:
                        act.wait_ge(y_done, n - 1)
                    for f in range(HID // P):
                        last_f = act.activation(
                            hid_t[:, m % 2, f, :], bank[2 + m % 2][:, f * P:(f + 1) * P], ACT.Relu,
                            bias=weights(m, WCOLS - HID // P + f, WCOLS - HID // P + f + 1))
                    last_f.then_inc(hid_ready, 1)
                    if m == BIAS_AT[2]:
                        act.wait_ge(combt_done, i + 1)
                        if not isinstance(i, int) or i >= 1:
                            act.wait_ge(bias_done, i)
                        act.copy(combine_t[:, :], combt_ps[:, 0:CHUNK // 2]).then_inc(combt_copied, 1)

            act.wait_ge(dispatched, 16 * K * TILES)
            for load in range(AHEAD):
                load_rows(load, load)
            relu_turn(0, False)
            with act.Fori(1, TURNS - 1) as i:
                relu_turn(i, False)
            relu_turn(TURNS - 1, True)

        @block.vector
        def _(dve):
            dve.wait_ge(consts_in, 16)
            dve.tensor_copy(tri[:, :], cst[:, C_TRI:C_TRI + P])
            dve.memset(ones[:, :], 1.0)
            dve.memset(eps[:, :], EPS).then_inc(small_ready, 1)
            for t in (count, room, shift, zero_e, expert_of, given, left, base):
                dve.memset(t[:, :], 0.0)
            dve.tensor_copy(rows_sb[:, :, :, D + 1], cst[:, C_DEST:C_DEST + K * TILES].rearrange(
                "p (k t) -> p k t", k=K)).then_inc(small_ready, 1)

            H_LAG = GROUP + 3
            steps = [0]

            def step(ins):
                steps[0] += 1
                ins.then_inc(h_step, 1)

            def settled():
                dve.wait_ge(h_step, steps[0])

            def h_tile_stats(c):
                step(dve.bn_stats(h_stats[:, c, :], x_sb[:, c, :]))

            def h_finish(c):
                dve.wait_ge(h_done, c + 1)
                dve.tensor_tensor(h_sb[:, c, :], bank[4 + c % 2][:, 0:D], b_bc[:, :], ALU.add).then_inc(h_ready, 1)

            for g in range(TILES // GROUP):
                dve.wait_ge(x_in[g], 16)
                if g == 1:
                    dve.wait_ge(gnn_w_in, 32)
                for i in range(GROUP):
                    h_tile_stats(g * GROUP + i)
                    if g * GROUP + i >= H_LAG:
                        h_finish(g * GROUP + i - H_LAG)
                settled()
                for i in range(GROUP):
                    last = dve.bn_aggr(h_mv[:, g * GROUP + i, :], h_stats[:, g * GROUP + i, :])
                last.then_inc(h_var, 1)
                dve.wait_ge(h_sqrt, g + 1)
                gs = slice(g * GROUP, (g + 1) * GROUP)
                step(dve.reciprocal(h_rstd[:, gs], h_sd[:, gs]))
                settled()
                for i in range(GROUP):
                    c = g * GROUP + i
                    dve.tensor_scalar(h_sb[:, c, :], x_sb[:, c, :], h_mv[:, c, 0:1], h_rstd[:, c:c + 1],
                                      ALU.subtract, ALU.mult).then_inc(xn_ready, 1)
            for c in range(TILES - H_LAG, TILES):
                h_finish(c)

            dve.wait_ge(router_w_in, 4 * 16)
            
            def bc(t, tiles):
                return t[:, :].rearrange("p (o e) -> p o e", o=1).to_broadcast([P, tiles, E])

            def by_tile(t, tiles):
                return t.rearrange("p (q o) -> p q o", o=1).to_broadcast([P, tiles, E])

            def route_chunk(j, first, tiles):
                done = [0]
                qs = slice(0, tiles)

                def rstep(ins):
                    done[0] += 1
                    ins.then_inc(r_step, 1)
                    return done[0]

                def after(n=None):
                    dve.wait_ge(r_step, R_STEPS * j + (n or done[0]))

                def carry_wait():
                    dve.tensor_copy(spare[0:1, 0:1], cst[0:1, 0:1])

                x1 = x_sb[:, bass.ds(first, tiles), :]
                dve.wait_ge(agg_back, j + 1)
                rstep(dve.tensor_tensor(x1, agg_ps[:, 0:tiles * D].rearrange("p (q d) -> p q d", d=D), x1, ALU.add))
                after()
                carry_wait()
                for q in range(tiles):
                    last = dve.bn_stats(stats[:, q, :], x_sb[:, bass.ds(first + q, 1), :])
                rstep(last)
                after()
                carry_wait()
                for q in range(tiles):
                    last = dve.bn_aggr(mv[:, q, :], stats[:, q, :])
                last.then_inc(var_ready, 1)
                dve.wait_ge(sd_ready, j + 1)
                rstep(dve.reciprocal(rstd[:, qs], sd[:, qs]))
                after()
                for q in range(tiles):
                    last = dve.tensor_scalar(xln[:, q:q + 1, :], x_sb[:, bass.ds(first + q, 1), :], mv[:, q, 0:1],
                                             rstd[:, q:q + 1], ALU.subtract, ALU.mult)
                last.then_inc(xln_ready, 1)
                dve.wait_ge(logits_done, j + 1)
                rstep(dve.tensor_tensor(logits[:, qs, :], logit_ps[:, 0:tiles * E].rearrange("p (q e) -> p q e", e=E),
                                        bc(br_bc, tiles), ALU.add))
                after()
                carry_wait()
                for q in range(tiles):
                    last = dve.max(top[:, q, :], logits[:, q, :])
                rstep(last)
                after()
                carry_wait()
                for q in range(tiles):
                    last = dve.max_index(top_at[:, q, :], top[:, q, :], logits[:, q, :])
                rstep(last)
                dve.tensor_tensor(gap[:, qs], top[:, qs, 1], top[:, qs, 0], ALU.subtract).then_inc(gap_ready, 1)
                after()
                rstep(dve.tensor_copy(top_f[:, :, qs], top_at[:, qs, 0:K].rearrange("p q k -> p k q")))
                after()
                for k in range(K):
                    last = dve.tensor_tensor(onehot[:, k, qs, :], bc(iota_e, tiles), by_tile(top_f[:, k, qs], tiles), ALU.is_equal)
                rstep(last)
                after()
                dve.tensor_tensor(chosen[:, qs, :], onehot[:, 0, qs, :], onehot[:, 1, qs, :], ALU.add).then_inc(chosen_ready, 1)
                dve.wait_ge(ex_ready, j + 1)
                rstep(dve.tensor_scalar_add(exp1[:, qs], ex[:, qs], 1.0))
                after()
                rstep(dve.reciprocal(gates[:, 0, qs], exp1[:, qs]))
                after()
                rstep(dve.tensor_tensor(gates[:, 1, qs], ex[:, qs], gates[:, 0, qs], ALU.mult))
                after()
                dve.tensor_copy(rows_sb[:, :, bass.ds(first, tiles), D], gates[:, :, qs]).then_inc(gates_set, 1)
                dve.wait_ge(rank_done, j + 1)
                ranks = rank_ps[:, 0:tiles * E].rearrange("p (q e) -> p q e", e=E)
                counted = rstep(dve.tensor_tensor(count_n[:, :], rank_ps[:, tiles * E:(tiles + 1) * E], count[:, :], ALU.add))
                rstep(dve.tensor_tensor(slot_a[:, qs, :], ranks, bc(left, tiles), ALU.is_ge))
                after(counted)
                padded = rstep(dve.tensor_scalar_add(room_i[:, 0, :], count_n[:, :], float(P - 1)))
                rstep(dve.tensor_tensor(slot_c[:, qs, :], ranks, bc(base, tiles), ALU.add))
                after(padded)
                rstep(dve.tensor_scalar(room_i[:, 1, :], room_i[:, 0, :], -P, None, ALU.bitwise_and))
                after()
                rstep(dve.tensor_copy(room_n[:, :], room_i[:, 1, :]))
                after()
                rstep(dve.tensor_tensor(added[:, :], room_n[:, :], room[:, :], ALU.subtract))
                after()
                rstep(dve.tensor_tensor_scan(ends[:, :], added[:, :], zero_e[:, :], given[:, 0:1], ALU.add, ALU.add))
                after()
                rstep(dve.tensor_tensor(shift_n[:, :], ends[:, :], room_n[:, :], ALU.subtract))
                after()
                rstep(dve.tensor_tensor(shift_d[:, :], shift_n[:, :], shift[:, :], ALU.subtract))
                after()
                rstep(dve.tensor_tensor(slot_b[:, qs, :], slot_a[:, qs, :], bc(shift_d, tiles), ALU.mult))
                after()
                rstep(dve.tensor_tensor(slot[:, qs, :], slot_c[:, qs, :], slot_b[:, qs, :], ALU.add))
                after()
                for k in range(K):
                    last = dve.tensor_tensor(weighted[:, k, qs, :], onehot[:, k, qs, :], slot[:, qs, :], ALU.mult)
                rstep(last)
                after()
                rstep(dve.reduce_sum(slot_k[:, :, qs], weighted[:, :, qs, :], axis=AX.X))
                after()
                dve.tensor_copy(slot_of[:, :, bass.ds(first, tiles)], slot_k[:, :, qs]).then_inc(slots_ready, 1)
                for k in range(K):
                    last = dve.tensor_tensor(weighted[:, k, qs, :], onehot[:, k, qs, :], by_tile(gates[:, k, qs], tiles), ALU.mult)
                rstep(last)
                rstep(dve.tensor_copy(count[:, :], count_n[:, :]))
                rstep(dve.tensor_copy(room[:, :], room_n[:, :]))
                rstep(dve.tensor_copy(given[:, :], ends[:, E - 1:E]))
                rstep(dve.tensor_tensor(left[:, :], room_n[:, :], count_n[:, :], ALU.subtract))
                rstep(dve.scalar_tensor_tensor(opened[:, :], added[:, :], 0.0, shift_d[:, :], ALU.is_gt, ALU.mult))
                after()
                rstep(dve.tensor_tensor(shift_n[:, :], opened[:, :], shift[:, :], ALU.add))
                rstep(dve.tensor_scalar(le[:, :], ends[:, :], block_start, 0.0, ALU.is_le, ALU.add, accum_out=le_n[:, :]))
                after()
                rstep(dve.tensor_copy(shift[:, :], shift_n[:, :]))
                rstep(dve.tensor_tensor(base[:, :], shift_n[:, :], count_n[:, :], ALU.add))
                rstep(dve.scalar_tensor_tensor(le_m[:, :], le_n[:, :], float(E), le_n[:, :], ALU.is_lt, ALU.mult))
                dve.tensor_tensor(combine[:, bass.ds(first, tiles), :], weighted[:, 0, qs, :], weighted[:, 1, qs, :],
                                  ALU.add).then_inc(combine_ready, 1)
                after()
                rstep(dve.tensor_tensor(expert_of[:, :], expert_of[:, :], le_m[:, :], ALU.add))
                after()
                assert done[0] == R_STEPS, done[0]

            with dve.Fori(0, WHOLE) as j:
                route_chunk(j, TPC * j, TPC)
            route_chunk(WHOLE, TPC * WHOLE, TAIL)
            dve.wait_ge(experts_turned, 1)
            dve.tensor_copy(expert_row[0:1, 0:TURN], expert_ps[0:1, 0:TURN]).then_inc(experts_known, 1)
            route_chunk(WHOLE + 1, TPC * WHOLE + TAIL, TAIL)
            dve.wait_ge(experts_turned, 2)
            dve.tensor_copy(expert_row[0:1, TURN:BLOCKS], expert_ps[0:1, TURN:BLOCKS]).then_inc(experts_known, 1)
            dve.wait_ge(combine_ready, CHUNKS)

            def copy_t(n, m):
                dve.wait_ge(xbt_done, n + 1)
                if not isinstance(n, int) or n >= 2:
                    dve.wait_ge(hid_done, n - 1)
                dve.tensor_copy(xb_t[:, m % 2, :], bank[m % 2][:, 0:P]).then_inc(xbt_copied, 1)

            def scale_turn(i, first, last):
                for m in range(TURN):
                    n = TURN * i + m
                    if not last or m + 2 < TURN:
                        copy_t(n + 2, m)
                    if m % QUAD == 0:
                        dve.wait_ge(xb_in[m // QUAD], 16 * (i + 1))
                        if not first:
                            for u in range(QUAD):
                                dve.wait_ge(y_out[m + u], 16 * i)
                        dve.tensor_scalar(y_to[:, m:m + QUAD], xb[:, m // QUAD, :, D + 1], -1.0, float(K * N), ALU.mult, ALU.add)
                    dve.wait_ge(y_done, n + 1)
                    dve.tensor_scalar(y_sb[:, m, :], bank[4 + m % 2][:, 0:D], xb[:, m // QUAD, m % QUAD, D:D + 1], None,
                                      ALU.mult).then_inc(y_ready, 1)
                    if m % QUAD == QUAD - 1:
                        dve.engine_nop().then_inc(xb_free, 1)
                    if isinstance(n, int) and n in SUM_AFTER:
                        finish(SUM_AFTER[n])
                    if m == BIAS_AT[0]:
                        if not first:
                            dve.wait_ge(combt_done, i)
                        dve.tensor_copy(staged[:, :, :], combine[:, bass.ds(i * TPC, TPC), :]).then_inc(gates_staged, 1)
                    if m == BIAS_AT[4]:
                        dve.wait_ge(bias_done, i + 1)
                        x1 = x_sb[:, bass.ds(i * TPC, TPC), :]
                        dve.tensor_tensor(x1, bias_ps[:, :].rearrange("p (q d) -> p q d", d=D), x1, ALU.add).then_inc(bias_added, 1)

            def finish(c):
                ts = slice(c * TPC, (c + 1) * TPC)
                dve.wait_ge(pairs_in[c], 16 * K)
                dve.wait_ge(bias_added, c + 1)
                dve.tensor_tensor(x_sb[:, ts, :], x_sb[:, ts, :], pairs_sb[:, 0, ts, :], ALU.add).then_inc(f_step, 1)
                dve.wait_ge(f_step, c + 1)
                dve.tensor_tensor(x_sb[:, ts, :], x_sb[:, ts, :], pairs_sb[:, 1, ts, :], ALU.add).then_inc(out_ready, 1)

            copy_t(0, 0)
            copy_t(1, 1)
            scale_turn(0, True, False)
            with dve.Fori(1, PLAIN) as i:
                scale_turn(i, False, False)
            for i in range(PLAIN, TURNS):
                scale_turn(i, False, i == TURNS - 1)
            for c in range(len(SUM_AFTER), OUTS):
                finish(c)

        @block.tensor
        def _(pe):
            def accumulate(s, bank_acc):
                for i in range(CPS):
                    c = s * CPS + i
                    last = pe.matmul(bank_acc[:, :], h_sb[:, c, :], adj_sb[:, s, i, :], start=(c == 0), stop=(c == TILES - 1))
                last.then_inc(adj_used, 1)

            pe.wait_ge(consts_in, 16)
            for c in range(TILES + 5):
                if c == 0:
                    pe.wait_ge(gnn_w_in, 32)
                if 2 <= c < TILES + 2:
                    t = c - 2
                    pe.wait_ge(xnt_copied, t + 1)
                    if t >= 2:
                        pe.wait_ge(h_ready, t - 1)
                    pe.matmul(bank[4 + t % 2][:, 0:D], xn_t[:, t % 2, :], wt[:, :], start=True, stop=True).then_inc(h_done, 1)
                if c >= 5:
                    t = c - 5
                    pe.wait_ge(h_ready, t + 1)
                    if t % CPS == 0:
                        pe.wait_ge(adj_in[t // CPS], 16)
                    last = pe.matmul(acc[0][:, :], h_sb[:, t, :], adj_sb[:, t // CPS, t % CPS, :], start=(t == 0), stop=(t == TILES - 1))
                    if t % CPS == CPS - 1:
                        last.then_inc(adj_used, 1)
                if c < TILES:
                    pe.wait_ge(xn_ready, c + 1)
                    pe.transpose(bank[c % 2][:, 0:P], h_sb[:, c, :], ident).then_inc(xnt_done, 1)

            def back(j, tiles):
                pe.wait_ge(agg_copied, j + 1)
                for q in range(tiles):
                    last = pe.transpose(agg_ps[:, q * P:(q + 1) * P], agg_t[:, q * P:(q + 1) * P], ident)
                last.then_inc(agg_back, 1)

            def turn_rows(j, tiles):
                pe.wait_ge(xln_ready, j + 1)
                for q in range(tiles):
                    last = pe.transpose(xlnt_ps[:, q * P:(q + 1) * P], xln[:, q, :], ident)
                last.then_inc(xlnt_done, 1)

            def route(j, tiles):
                pe.wait_ge(xlnt_copied, j + 1)
                for q in range(tiles):
                    last = pe.matmul(logit_ps[:, q * E:(q + 1) * E], xln_t[:, q * P:(q + 1) * P], wr[:, :], start=True, stop=True)
                last.then_inc(logits_done, 1)

            def count_ranks(j, tiles):
                pe.wait_ge(chosen_ready, j + 1)
                for q in range(tiles + 1):
                    for r in range(min(q + 1, tiles)):
                        last = pe.matmul(rank_ps[:, q * E:(q + 1) * E], (tri if r == q else ones)[:, :], chosen[:, r, :],
                                         start=(r == 0), stop=(r == min(q, tiles - 1)))
                last.then_inc(rank_done, 1)

            def turn_experts(chunks):
                pe.wait_ge(r_step, R_STEPS * chunks)
                if chunks == CHUNKS:
                    pe.wait_ge(experts_known, 1)
                pe.matmul(expert_ps[0:1, 0:BLOCKS], expert_of[:, 0:1], ident, start=True, stop=True).then_inc(experts_turned, 1)

            def chunk(j, par):
                for s in range(SLOTS):
                    pe.wait_ge(adj_in[s], 16 * (j + 1))
                    accumulate(s, acc[par])
                    if s in (0, 2, 3, 5):
                        {0: back, 2: turn_rows, 3: route, 5: count_ranks}[s](j - 1, TPC)

            def tail_chunk(c, tiles_before, places):
                j = WHOLE + c
                for t in range(TILES):
                    s = c * SLOTS // 2 + t // (2 * CPS)
                    if t % (2 * CPS) == 0:
                        pe.wait_ge(adj_in[s], 16 * (WHOLE + 1))
                    last = pe.matmul(acc[j % 2][:, 0:TAIL * P], h_sb[:, t, :], tail_sb[:, s, t % (2 * CPS), :],
                                     start=(t == 0), stop=(t == TILES - 1))
                    if t % (2 * CPS) == 2 * CPS - 1:
                        last.then_inc(adj_used, 1)
                    if t in places:
                        (back, turn_rows, route, count_ranks)[places.index(t)](j - 1, tiles_before)

            pe.wait_ge(router_w_in, 4 * 16)
            pe.wait_ge(small_ready, 2)
            with pe.Fori(0, (WHOLE - 1) // 2) as jj:
                chunk(2 * jj + 1, 1)
                chunk(2 * jj + 2, 0)
            tail_chunk(0, TPC, (2, 11, 13, 21))
            tail_chunk(1, TAIL, (2, 13, 15, 21))
            turn_experts(CHUNKS - 1)
            for piece in (back, turn_rows, route, count_ranks):
                piece(CHUNKS - 1, TAIL)
            turn_experts(CHUNKS)

            def turn_block(i, m):
                n = TURN * i + m
                if m % QUAD == 0:
                    pe.wait_ge(xb_in[m // QUAD], 16 * (i + 1))
                pe.transpose(bank[m % 2][:, 0:P], xb[:, m // QUAD, m % QUAD, 0:D], ident).then_inc(xbt_done, 1)

            def first_layer(i, m):
                n = TURN * i + m
                pe.wait_ge(wb_in[m], 16 * (i + 1))
                pe.wait_ge(xbt_copied, n + 1)
                for f in range(HID // P):
                    last = pe.matmul(bank[2 + m % 2][:, f * P:(f + 1) * P], weights(m, f * P, (f + 1) * P), xb_t[:, m % 2, :],
                                     start=True, stop=True)
                last.then_inc(hid_done, 1)

            def second_layer(i, m):
                n = TURN * i + m
                pe.wait_ge(hid_ready, n + 1)
                if not isinstance(n, int) or n >= 2:
                    pe.wait_ge(y_ready, n - 1)
                for f in range(HID // P):
                    last = pe.matmul(bank[4 + m % 2][:, 0:D], hid_t[:, m % 2, f, :], weights(m, HID + f * D, HID + (f + 1) * D),
                                     start=(f == 0), stop=(f == HID // P - 1))
                last.then_inc(y_done, 1)

            def turn_gates(i):
                pe.wait_ge(gates_staged, i + 1)
                for h in range(TPC // 2):
                    last = pe.transpose(combt_ps[:, h * P:(h + 1) * P], staged[:, 2 * h:2 * h + 2, :].rearrange("p q e -> p (q e)"),
                                        ident)
                last.then_inc(combt_done, 1)

            def second_bias(i):
                pe.wait_ge(combt_copied, i + 1)
                if not isinstance(i, int) or i >= 1:
                    pe.wait_ge(bias_added, i)
                for h in range(TPC // 2):
                    last = pe.matmul(bias_ps[:, 2 * h * D:2 * (h + 1) * D], combine_t[:, h * P:(h + 1) * P],
                                     b2_sb[:, :, :].rearrange("p h d -> p (h d)"), start=True, stop=True)
                last.then_inc(bias_done, 1)

            def expert_turn(i, last):
                for m in range(TURN):
                    if m == BIAS_AT[1]:
                        turn_gates(i)
                    if m == BIAS_AT[3]:
                        second_bias(i)
                    if not last or m + 2 < TURN:
                        turn_block(i + (m + 2) // TURN, (m + 2) % TURN)
                    if not last or m + 1 < TURN:
                        first_layer(i + (m + 1) // TURN, (m + 1) % TURN)
                    second_layer(i, m)

            pe.wait_ge(experts_known, 2)
            turn_block(0, 0)
            turn_block(0, 1)
            first_layer(0, 0)
            expert_turn(0, False)
            with pe.Fori(1, TURNS - 1) as i:
                expert_turn(i, False)
            expert_turn(TURNS - 1, True)


def kernel(x, adj, L0_gnn_W, L0_gnn_b, L0_ffn_Wr, L0_ffn_br, L0_ffn_W1, L0_ffn_b1, L0_ffn_W2, L0_ffn_b2):
    import numpy as np
    import concourse.bacc as bacc
    from concourse.bass_utils import run_bass_kernel_spmd

    adj = np.asarray(adj)
    adj_t = adj[:WHOLE * CHUNK].reshape(WHOLE, CHUNK, TILES, P).transpose(0, 3, 2, 1)
    adj_tail = adj[WHOLE * CHUNK:].reshape(2, TAIL * P, TILES, P).transpose(0, 3, 2, 1)
    w1 = np.asarray(L0_ffn_W1)
    w2 = np.asarray(L0_ffn_W2).reshape(E, HID // P, P, D).transpose(0, 2, 1, 3).reshape(E, P, HID // P * D)
    b1 = np.asarray(L0_ffn_b1).reshape(E, HID // P, P).transpose(0, 2, 1)
    consts = np.zeros((P, C_COLS), np.float32)
    consts[:, C_ID:C_ID + P] = np.eye(P)
    consts[:, C_TRI:C_TRI + P] = np.triu(np.ones((P, P)), 1)
    consts[:, C_IOTA:C_IOTA + E] = np.arange(E)
    consts[:, C_DEST:C_BLK] = K * N - (np.arange(K * TILES)[None, :] * P + np.arange(P)[:, None])
    consts[:, C_BLK] = np.arange(P) * P
    ins = {
        "x": x, "adj_t": adj_t, "adj_tail": adj_tail, "w_t": np.asarray(L0_gnn_W).T, "b": L0_gnn_b, "w_router": L0_ffn_Wr,
        "b_router": L0_ffn_br, "w_experts": np.concatenate([w1, w2, b1], axis=2), "b2": L0_ffn_b2, "consts": consts,
    }
    ins = {name: np.ascontiguousarray(a) for name, a in ins.items()}
    nc = bacc.Bacc("TRN2", target_bir_lowering=False, num_devices=1)
    F32 = mybir.dt.float32
    args = {name: nc.dram_tensor(name, a.shape, F32, kind="ExternalInput").ap() for name, a in ins.items()}
    out = nc.dram_tensor("out", [N, D], F32, kind="ExternalOutput").ap()
    gnn_moe(nc, **args, out=out)
    r = run_bass_kernel_spmd(nc, [ins], core_ids=[0])
    return r.results[0]["out"]
```

```python
import concourse.bass as bass
from concourse import mybir
from contextlib import ExitStack

P = 128
N = 4096
D = 128
HID = 256
E = 64
K = 2
EPS = 1e-5
R_STEPS = 37
TILES = N // P
TPC = 4
CHUNK = TPC * P
WHOLE = TILES // TPC - 1
TAIL = TPC // 2
CHUNKS = WHOLE + 2
SLOTS = 8
CPS = TILES // SLOTS
OUTS = TILES // TPC
GROUP = 4
N_AHEAD = 2
G_LAG = 2 * GROUP
BLOCKS = (N * K + E * (P - 1)) // P + 1
TURN = 32
YRING = 16
RINGS = TURN // YRING
QUAD = 4
QUADS = YRING // QUAD
WB_SLOTS = 10
LOOKUP = 8
ROWS = BLOCKS * P
RW = D + 2
WCOLS = HID + HID // P * D + HID // P
C_ID, C_TRI, C_IOTA, C_DEST, C_BLK = 0, P, 2 * P, 2 * P + E, 2 * P + E + K * TILES
C_COLS = C_BLK + 1
TURNS = BLOCKS // TURN
PAIRS = 2
LATE = OUTS - 2 * PAIRS
DONE_AT = [(c + 1) * K * CHUNK // P + E for c in range(OUTS)]
assert DONE_AT[-1] == BLOCKS
BIAS_AT = (1, 4, 5, 9, 11)
SUM_PARTS = 4
SUM_AT = [max(n + 11, BLOCKS - TURN + 2 * SUM_PARTS + SUM_PARTS * c) for c, n in enumerate(DONE_AT)]
SUM_AFTER = {at + part: (c, part) for c, at in enumerate(SUM_AT) for part in range(SUM_PARTS) if at + SUM_PARTS <= BLOCKS}
STORED_TO = {c: sum(at + SUM_PARTS < n + 5 for at in SUM_AT) for c, n in enumerate(DONE_AT)}
assert BLOCKS == 128 and BLOCKS % TURN == 0 and TURNS == LATE


def gnn_moe(nc, x, adj_t, adj_tail, w_t, b, w_router, b_router, w_experts, b2, consts, out):
    F32, BF16 = mybir.dt.float32, mybir.dt.bfloat16
    I32, U32 = mybir.dt.int32, mybir.dt.uint32
    ALU, ACT, AX = mybir.AluOpType, mybir.ActivationFunctionType, mybir.AxisListType

    rows_dram = nc.dram_tensor("dispatched_rows", [ROWS, RW], F32)
    pair_out = nc.dram_tensor("pair_out", [K * N, D], F32)

    with ExitStack() as ctx:
        def sb(name, shape, dt=F32):
            return ctx.enter_context(nc.sbuf_tensor(name, shape, dt))

        def ps(name, shape=(P, 512)):
            return ctx.enter_context(nc.psum_tensor(name, list(shape), F32))

        def sem(name):
            return ctx.enter_context(nc.semaphore(name))

        cst = sb("cst", [P, C_COLS])
        ident = cst[:, C_ID:C_ID + P]
        iota_e = cst[:, C_IOTA:C_IOTA + E]
        block_start = cst[:, C_BLK:C_BLK + 1]
        tri = sb("tri", [P, P], BF16)
        ones = sb("ones", [P, P], BF16)
        eps = sb("eps", [P, 1])
        spare = sb("spare", [1, 1])
        early_root = sb("early_root", [P, 1])
        wt = sb("wt", [P, D])
        b_bc = sb("b_bc", [P, D])
        wr = sb("wr", [P, E])
        br_bc = sb("br_bc", [P, E])
        b2_sb = sb("b2_sb", [2 * E, 2, D])
        zeros = sb("zeros", [P, 16 * RW])
        x_sb = sb("x_sb", [P, TILES, D])
        h_sb = sb("h_sb", [P, TILES, D])
        adj_sb = sb("adj_sb", [P, SLOTS, CPS, CHUNK])
        xn_t = sb("xn_t", [P, 2, P])
        h_stats = sb("h_stats", [P, TILES, 6])
        h_mv = sb("h_mv", [P, TILES, 2])
        h_rstd = sb("h_rstd", [P, TILES])
        h_sd = sb("h_sd", [P, TILES])
        agg_t = sb("agg_t", [P, CHUNK])
        stats = sb("stats", [P, TPC, 6])
        mv = sb("mv", [P, TPC, 2])
        sd = sb("sd", [P, TPC])
        rstd = sb("rstd", [P, TPC])
        xln = sb("xln", [P, TPC, D])
        xln_t = sb("xln_t", [P, CHUNK])
        logits = sb("logits", [P, TPC, E])
        top = sb("top", [P, TPC, 8])
        top_at = sb("top_at", [P, TPC, 8], U32)
        top_f = sb("top_f", [P, K, TPC])
        gap = sb("gap", [P, TPC])
        ex = sb("ex", [P, TPC])
        exp1 = sb("exp1", [P, TPC])
        gates = sb("gates", [P, K, TPC])
        onehot = sb("onehot", [P, K, TPC, E])
        chosen = sb("chosen", [P, TPC, E], BF16)
        weighted = sb("weighted", [P, K, TPC, E])
        combine = sb("combine", [P, TILES, E])
        staged = sb("staged", [P, TPC, E])
        combine_t = sb("combine_t", [P, CHUNK])
        slot = sb("slot", [P, TPC, E])
        slot_a = sb("slot_a", [P, TPC, E])
        slot_b = sb("slot_b", [P, TPC, E])
        slot_c = sb("slot_c", [P, TPC, E])
        slot_k = sb("slot_k", [P, K, TPC])
        slot_of = sb("slot_of", [P, K, TILES], U32)
        count = sb("count", [P, E])
        count_n = sb("count_n", [P, E])
        room = sb("room", [P, E])
        room_n = sb("room_n", [P, E])
        room_i = sb("room_i", [P, 2, E], I32)
        added = sb("added", [P, E])
        ends = sb("ends", [P, E])
        given = sb("given", [P, 1])
        shift = sb("shift", [P, E])
        shift_n = sb("shift_n", [P, E])
        shift_d = sb("shift_d", [P, E])
        left = sb("left", [P, E])
        base = sb("base", [P, E])
        opened = sb("opened", [P, E])
        zero_e = sb("zero_e", [P, E])
        le = sb("le", [P, E])
        le_n = sb("le_n", [P, 1])
        le_m = sb("le_m", [P, 1])
        expert_of = sb("expert_of", [P, 1])
        expert_row = sb("expert_row", [1, BLOCKS], I32)
        rows_sb = sb("rows_sb", [P, K, TILES, RW])
        xb = sb("xb", [P, QUADS, QUAD, RW])
        wb = sb("wb", [P, WB_SLOTS, WCOLS])
        xb_t = sb("xb_t", [P, 2, P])
        hid_t = sb("hid_t", [P, 2, HID // P, P])
        y_sb = h_sb
        y_to = sb("y_to", [P, YRING], U32)
        adj_flat = adj_sb[:, :, :, :].rearrange("p s c n -> p (s c n)")
        adj_half = SLOTS // 2 * CPS * CHUNK
        pairs_sb = adj_flat[:, adj_half:adj_half + K * TILES * D].rearrange("p (k t d) -> p k t d", k=K, d=D)
        in_adj, in_zeros, in_h = adj_half // WCOLS, 16 * RW // WCOLS, (TILES - YRING) * D // WCOLS
        homes = [(wb[:, :, :].rearrange("p s w -> p (s w)"), i) for i in range(WB_SLOTS)] + [
            (adj_flat[:, 0:adj_half], i) for i in range(in_adj)] + [(zeros[:, :], i) for i in range(in_zeros)] + [
            (h_sb[:, YRING:TILES, :].rearrange("p t d -> p (t d)"), i) for i in range(in_h)]
        assert len(homes) == TURN

        def weights(m, a, b):
            home, at = homes[m]
            return home[:, at * WCOLS + a:at * WCOLS + b]

        tail_sb = adj_sb[:, :, :, :].rearrange("p s c n -> p s (c n)").rearrange("p s (c n) -> p s c n", n=TAIL * P)

        acc = [ps(f"acc{i}") for i in range(2)]
        bank = [ps(f"bank{i}") for i in range(6)]
        agg_ps, xlnt_ps, logit_ps, rank_ps, expert_ps = bank[0:5]
        h_ps = bank[4:6]
        combt_ps, bias_banks = acc[0], (acc[1], bank[5])

        consts_in, gnn_w_in, router_w_in = sem("consts_in"), sem("gnn_w_in"), sem("router_w_in")
        x_in = [sem(f"x_in{g}") for g in range(TILES // GROUP)]
        small_ready = sem("small_ready")
        adj_in = [sem(f"adj_in{s}") for s in range(SLOTS)]
        adj_used = sem("adj_used")
        b2_zeroed, zeros_set, rows_zeroed = sem("b2_zeroed"), sem("zeros_set"), sem("rows_zeroed")
        h_step, h_var, h_sqrt, xn_ready = sem("h_step"), sem("h_var"), sem("h_sqrt"), sem("xn_ready")
        xnt_done, xnt_copied, h_done, h_ready = sem("xnt_done"), sem("xnt_copied"), sem("h_done"), sem("h_ready")
        agg_copied, agg_back = sem("agg_copied"), sem("agg_back")
        r_step, var_ready, sd_ready = sem("r_step"), sem("var_ready"), sem("sd_ready")
        xln_ready, xlnt_done, xlnt_copied = sem("xln_ready"), sem("xlnt_done"), sem("xlnt_copied")
        logits_done, gap_ready, ex_ready = sem("logits_done"), sem("gap_ready"), sem("ex_ready")
        chosen_ready, rank_done, combine_ready = sem("chosen_ready"), sem("rank_done"), sem("combine_ready")
        combt_done, combt_copied, bias_done = sem("combt_done"), sem("combt_copied"), sem("bias_done")
        gates_staged = sem("gates_staged")
        bias_added, rows_copied, slots_ready, gates_set = (
            sem("bias_added"), sem("rows_copied"), sem("slots_ready"), sem("gates_set"))
        dispatched = sem("dispatched")
        experts_turned, experts_known = sem("experts_turned"), sem("experts_known")
        xb_in = [sem(f"xb_in{s}") for s in range(QUADS)]
        xb_free = sem("xb_free")
        wb_in = [sem(f"wb_in{s}") for s in range(TURN)]
        xbt_done, xbt_copied, hid_done, hid_ready = sem("xbt_done"), sem("xbt_copied"), sem("hid_done"), sem("hid_ready")
        y_done, y_ready = sem("y_done"), sem("y_ready")
        y_out = [sem(f"y_out{s}") for s in range(YRING)]
        pairs_in = [sem(f"pairs_in{i}") for i in range(OUTS)]
        f_step, stored = sem("f_step"), sem("stored")

        block = ctx.enter_context(nc.Block())

        @block.sync
        def _(sp):
            xv = x.rearrange("(t p) d -> p t d", p=P)
            for g in range(TILES // GROUP):
                sp.dma_start(x_sb[:, g * GROUP:(g + 1) * GROUP, :], xv[:, g * GROUP:(g + 1) * GROUP, :]).then_inc(x_in[g], 16)
                if g == 0:
                    sp.dma_start(cst[:, :], consts).then_inc(consts_in, 16)
                if g == 1:
                    sp.dma_start(wt[:, :], w_t).then_inc(gnn_w_in, 16)
                    sp.dma_start(b_bc[:, :], b.rearrange("(o d) -> o d", o=1).to_broadcast([P, D])).then_inc(gnn_w_in, 16)
            for s in range(SLOTS):
                sp.dma_start(adj_sb[:, s, :, :], adj_t[0, :, s * CPS:(s + 1) * CPS, :]).then_inc(adj_in[s], 16)
            sp.dma_start(wr[:, :], w_router).then_inc(router_w_in, 16)
            sp.dma_start(br_bc[:, :], b_router.rearrange("(o d) -> o d", o=1).to_broadcast([P, E])).then_inc(router_w_in, 16)
            sp.wait_ge(b2_zeroed, 1)
            for half in range(2):
                sp.dma_start(b2_sb[half * E:(half + 1) * E, half, :], b2).then_inc(router_w_in, 16)
            rows_z = rows_dram.ap().rearrange("(z p r) c -> z p (r c)", p=P, r=16)

            def load_chunk(j, zero_part):
                for s in range(SLOTS):
                    sp.wait_ge(adj_used, (j - 1) * SLOTS + s + 1)
                    sp.dma_start(adj_sb[:, s, :, :], adj_t[bass.ds(j, 1), :, s * CPS:(s + 1) * CPS, :].rearrange(
                        "o p c n -> p (o c) n")).then_inc(adj_in[s], 16)
                    if zero_part is not None and s % 2 == 1 and s < 7:
                        z = zero_part * 3 + s // 2
                        if z < rows_z.shape[0]:
                            if z == 0:
                                sp.wait_ge(zeros_set, 1)
                            sp.dma_start(rows_z[z], zeros[:, :]).then_inc(rows_zeroed, 16)

            for j in range(1, 4):
                load_chunk(j, j - 1)
            with sp.Fori(4, WHOLE) as j:
                load_chunk(j, None)
            for c in range(2):
                for h in range(SLOTS // 2):
                    s = c * SLOTS // 2 + h
                    sp.wait_ge(adj_used, (WHOLE - 1) * SLOTS + s + 1)
                    sp.dma_start(tail_sb[:, s, :, :], adj_tail[c, :, h * 2 * CPS:(h + 1) * 2 * CPS, :]).then_inc(adj_in[s], 16)

            pv = pair_out.ap().rearrange("(k t p) d -> p k t d", k=K, p=P)
            ov = out.rearrange("(t p) d -> p t d", p=P)

            def load_pairs(c):
                for m in range(YRING):
                    sp.wait_ge(y_out[m], 16 * (DONE_AT[c] // YRING + (m < DONE_AT[c] % YRING)))
                ts = slice(c * TPC, (c + 1) * TPC)
                for k in range(K):
                    sp.dma_start(pairs_sb[:, k, ts, :], pv[:, k, ts, :]).then_inc(pairs_in[c], 16)

            def store(c):
                ts = slice(c * TPC, (c + 1) * TPC)
                sp.wait_ge(f_step, SUM_PARTS * (c + 1))
                sp.dma_start(ov[:, ts, :], x_sb[:, ts, :]).then_inc(stored, 16)

            def load_turn(i):
                for m in range(TURN):
                    n = TURN * i + m
                    if m % LOOKUP == 0:
                        _, experts = nc.values_load_multi_w_load_instructions(
                            expert_row[0:1, bass.ds(n, LOOKUP)], engines=[mybir.EngineType.SP], min_val=0, max_val=E - 1,
                            skip_runtime_bounds_check_because="VectorE compares them with E as it makes them")
                    if isinstance(n, int) and n == TURN - in_h:
                        sp.wait_ge(adj_used, SLOTS * (WHOLE + 1))
                    if not isinstance(n, int) or n >= TURN:
                        sp.wait_ge(y_done, n - TURN + 1)
                    sp.dma_start(weights(m, 0, WCOLS), w_experts[bass.ds(experts[m % LOOKUP], 1), :, :].rearrange(
                        "o p c -> p (o c)")).then_inc(wb_in[m], 16)

            sp.wait_ge(experts_known, 1)
            sp.wait_ge(rows_zeroed, 16 * 8)
            sp.wait_ge(adj_used, SLOTS * WHOLE + SLOTS // 2)
            load_turn(0)
            sp.wait_ge(experts_known, 2)
            with sp.Fori(1, TURNS - 1) as i:
                load_turn(i)
            load_turn(TURNS - 1)
            stores = 0
            for c in range(OUTS):
                load_pairs(c)
                while stores < STORED_TO[c]:
                    store(stores)
                    stores += 1
            for c in range(stores, OUTS):
                store(c)
            sp.wait_ge(stored, 16 * OUTS)

        @block.gpsimd
        def _(pool):
            pool.memset(b2_sb[:, :, :], 0.0).then_inc(b2_zeroed, 1)
            pool.memset(zeros[:, :], 0.0).then_inc(zeros_set, 1)
            pool.wait_ge(rows_zeroed, 16 * 8)
            for j in range(CHUNKS):
                pool.wait_ge(slots_ready, j + 1)
                pool.wait_ge(gates_set, j + 1)
                pool.wait_ge(rows_copied, j + 1)
                first, tiles = (j * TPC, TPC) if j < WHOLE else (WHOLE * TPC + (j - WHOLE) * TAIL, TAIL)
                for t in range(first, first + tiles):
                    for k in range(K):
                        pool.indirect_dma_start(
                            out=rows_dram[:, :], out_offset=bass.IndirectOffsetOnAxis(ap=slot_of[:, k, t:t + 1], axis=0),
                            in_=rows_sb[:, k, t, :], in_offset=None, bounds_check=ROWS - 1,
                            oob_is_err=False).then_inc(dispatched, 16)
            for n in range(BLOCKS):
                m = n % YRING
                pool.wait_ge(y_ready, n + 1)
                pool.indirect_dma_start(
                    out=pair_out[:, :], out_offset=bass.IndirectOffsetOnAxis(ap=y_to[:, m:m + 1], axis=0),
                    in_=y_sb[:, m, :], in_offset=None, bounds_check=K * N - 1, oob_is_err=False).then_inc(y_out[m], 16)

        @block.scalar
        def _(act):
            def root(g):
                gs = slice(g * GROUP, (g + 1) * GROUP)
                act.wait_ge(h_var, g + 1)
                act.activation(h_sd[:, gs], h_mv[:, gs, 1], ACT.Sqrt, bias=eps[:, 0:1]).then_inc(h_sqrt, 1)

            act.wait_ge(small_ready, 1)
            act.activation(early_root[:, :], eps[:, :], ACT.Sqrt)
            for g in range(N_AHEAD):
                root(g)
            for c in range(TILES):
                act.wait_ge(xnt_done, c + 1)
                if c >= 2:
                    act.wait_ge(h_done, c - 1)
                act.copy(xn_t[:, c % 2, :], bank[c % 2][:, 0:P]).then_inc(xnt_copied, 1)
                if c % GROUP == GROUP - 1 and c // GROUP + N_AHEAD < TILES // GROUP:
                    root(c // GROUP + N_AHEAD)

            def chunk(j, par, first, tiles):
                used = SLOTS * (j + 1) if tiles == TPC else SLOTS * WHOLE + SLOTS // 2 * (j - WHOLE + 1)
                act.wait_ge(adj_used, used)
                act.copy(agg_t[:, 0:tiles * P], acc[par][:, 0:tiles * P]).then_inc(agg_copied, 1)
                act.wait_ge(var_ready, j + 1)
                act.activation(sd[:, 0:tiles], mv[:, 0:tiles, 1], ACT.Sqrt, bias=eps[:, 0:1]).then_inc(sd_ready, 1)
                act.wait_ge(xlnt_done, j + 1)
                act.copy(xln_t[:, 0:tiles * P], xlnt_ps[:, 0:tiles * P]).then_inc(xlnt_copied, 1)
                for k in range(K):
                    last = act.copy(rows_sb[:, k, bass.ds(first, tiles), 0:D], xln[:, 0:tiles, :])
                last.then_inc(rows_copied, 1)
                act.wait_ge(gap_ready, j + 1)
                act.activation(ex[:, 0:tiles], gap[:, 0:tiles], ACT.Exp).then_inc(ex_ready, 1)

            with act.Fori(0, (WHOLE - 1) // 2) as jj:
                for par in range(2):
                    chunk(2 * jj + par, par, TPC * (2 * jj + par), TPC)
            chunk(WHOLE - 1, (WHOLE - 1) % 2, TPC * (WHOLE - 1), TPC)
            for c in range(2):
                chunk(WHOLE + c, (WHOLE + c) % 2, TPC * WHOLE + TAIL * c, TAIL)

            for p in range(PAIRS):
                act.wait_ge(combt_done, p + 1)
                if p >= 1:
                    act.wait_ge(bias_done, p)
                act.copy(combine_t[:, :], combt_ps[:, :]).then_inc(combt_copied, 1)

            rows_v = rows_dram.ap().rearrange("(l u p) c -> l p u c", u=QUAD, p=P)
            AHEAD = QUADS - 1

            def load_rows(load, slot):
                act.dma_start(xb[:, slot, :, :], rows_v[bass.ds(load, 1), :, :, :].rearrange(
                    "o p u c -> p (o u) c")).then_inc(xb_in[slot], 16)

            def relu_turn(i, last):
                for m in range(TURN):
                    n = TURN * i + m
                    q = m // QUAD
                    if m % QUAD == 3 and (not last or q + AHEAD < RINGS * QUADS):
                        load = RINGS * QUADS * i + q + AHEAD
                        if not isinstance(load, int) or load >= QUADS:
                            act.wait_ge(xb_free, load - QUADS + 1)
                        load_rows(load, (q + AHEAD) % QUADS)
                    act.wait_ge(wb_in[m], 16 * (i + 1))
                    act.wait_ge(hid_done, n + 1)
                    if not isinstance(n, int) or n >= 2:
                        act.wait_ge(y_done, n - 1)
                    for f in range(HID // P):
                        last_f = act.activation(
                            hid_t[:, m % 2, f, :], bank[2 + m % 2][:, f * P:(f + 1) * P], ACT.Relu,
                            bias=weights(m, WCOLS - HID // P + f, WCOLS - HID // P + f + 1))
                    last_f.then_inc(hid_ready, 1)
                    if m == BIAS_AT[2]:
                        act.wait_ge(combt_done, PAIRS + i + 1)
                        act.wait_ge(bias_done, PAIRS + i)
                        act.copy(combine_t[:, 0:CHUNK // 2], combt_ps[:, 0:CHUNK // 2]).then_inc(combt_copied, 1)

            act.wait_ge(dispatched, 16 * K * TILES)
            for load in range(AHEAD):
                load_rows(load, load)
            relu_turn(0, False)
            with act.Fori(1, TURNS - 1) as i:
                relu_turn(i, False)
            relu_turn(TURNS - 1, True)

        @block.vector
        def _(dve):
            dve.memset(eps[:, :], EPS).then_inc(small_ready, 1)

            steps = [0]

            def step(ins):
                steps[0] += 1
                ins.then_inc(h_step, 1)

            def settled():
                dve.wait_ge(h_step, steps[0])

            def normalise(g):
                tiles = range(g * GROUP, (g + 1) * GROUP)
                dve.wait_ge(x_in[g], 16)
                for c in tiles:
                    last = dve.bn_stats(h_stats[:, c, :], x_sb[:, c, :])
                step(last)
                settled()
                for c in tiles:
                    last = dve.bn_aggr(h_mv[:, c, :], h_stats[:, c, :])
                last.then_inc(h_var, 1)
                if g == 0:
                    small_work()
                dve.wait_ge(h_sqrt, g + 1)
                gs = slice(g * GROUP, (g + 1) * GROUP)
                step(dve.reciprocal(h_rstd[:, gs], h_sd[:, gs]))
                settled()
                for c in tiles:
                    dve.tensor_scalar(h_sb[:, c, :], x_sb[:, c, :], h_mv[:, c, 0:1], h_rstd[:, c:c + 1],
                                      ALU.subtract, ALU.mult).then_inc(xn_ready, 1)

            def small_work():
                for t in (count, room, shift, zero_e, expert_of, given, left, base):
                    dve.memset(t[:, :], 0.0)
                dve.memset(ones[:, :], 1.0)

            def from_consts():
                dve.wait_ge(consts_in, 16)
                dve.tensor_copy(tri[:, :], cst[:, C_TRI:C_TRI + P])
                dve.tensor_copy(rows_sb[:, :, :, D + 1], cst[:, C_DEST:C_DEST + K * TILES].rearrange(
                    "p (k t) -> p k t", k=K)).then_inc(small_ready, 1)

            def finish_h(g):
                if g == 0:
                    dve.wait_ge(gnn_w_in, 32)
                dve.wait_ge(h_done, (g + 1) * GROUP)
                dve.tensor_tensor(h_sb[:, g * GROUP:(g + 1) * GROUP, :], h_ps[g % 2][:, :].rearrange("p (q d) -> p q d", d=D),
                                  b_bc[:, :].rearrange("p (o d) -> p o d", o=1).to_broadcast([P, GROUP, D]),
                                  ALU.add).then_inc(h_ready, 1)

            for g in range(TILES // GROUP + N_AHEAD):
                if g < TILES // GROUP:
                    normalise(g)
                if g == N_AHEAD - 1:
                    from_consts()
                if g >= N_AHEAD:
                    finish_h(g - N_AHEAD)

            dve.wait_ge(router_w_in, 4 * 16)

            def bc(t, tiles):
                return t[:, :].rearrange("p (o e) -> p o e", o=1).to_broadcast([P, tiles, E])

            def by_tile(t, tiles):
                return t.rearrange("p (q o) -> p q o", o=1).to_broadcast([P, tiles, E])

            def route_chunk(j, first, tiles):
                done = [0]
                qs = slice(0, tiles)

                def rstep(ins):
                    done[0] += 1
                    ins.then_inc(r_step, 1)
                    return done[0]

                def after(n=None):
                    dve.wait_ge(r_step, R_STEPS * j + (n or done[0]))

                def carry_wait():
                    dve.tensor_copy(spare[0:1, 0:1], cst[0:1, 0:1])

                x1 = x_sb[:, bass.ds(first, tiles), :]
                dve.wait_ge(agg_back, j + 1)
                rstep(dve.tensor_tensor(x1, agg_ps[:, 0:tiles * D].rearrange("p (q d) -> p q d", d=D), x1, ALU.add))
                after()
                carry_wait()
                for q in range(tiles):
                    last = dve.bn_stats(stats[:, q, :], x_sb[:, bass.ds(first + q, 1), :])
                rstep(last)
                after()
                carry_wait()
                for q in range(tiles):
                    last = dve.bn_aggr(mv[:, q, :], stats[:, q, :])
                last.then_inc(var_ready, 1)
                dve.wait_ge(sd_ready, j + 1)
                rstep(dve.reciprocal(rstd[:, qs], sd[:, qs]))
                after()
                for q in range(tiles):
                    last = dve.tensor_scalar(xln[:, q:q + 1, :], x_sb[:, bass.ds(first + q, 1), :], mv[:, q, 0:1],
                                             rstd[:, q:q + 1], ALU.subtract, ALU.mult)
                last.then_inc(xln_ready, 1)
                dve.wait_ge(logits_done, j + 1)
                rstep(dve.tensor_tensor(logits[:, qs, :], logit_ps[:, 0:tiles * E].rearrange("p (q e) -> p q e", e=E),
                                        bc(br_bc, tiles), ALU.add))
                after()
                carry_wait()
                for q in range(tiles):
                    last = dve.max(top[:, q, :], logits[:, q, :])
                rstep(last)
                after()
                carry_wait()
                for q in range(tiles):
                    last = dve.max_index(top_at[:, q, :], top[:, q, :], logits[:, q, :])
                rstep(last)
                dve.tensor_tensor(gap[:, qs], top[:, qs, 1], top[:, qs, 0], ALU.subtract).then_inc(gap_ready, 1)
                after()
                rstep(dve.tensor_copy(top_f[:, :, qs], top_at[:, qs, 0:K].rearrange("p q k -> p k q")))
                after()
                for k in range(K):
                    last = dve.tensor_tensor(onehot[:, k, qs, :], bc(iota_e, tiles), by_tile(top_f[:, k, qs], tiles), ALU.is_equal)
                rstep(last)
                after()
                dve.tensor_tensor(chosen[:, qs, :], onehot[:, 0, qs, :], onehot[:, 1, qs, :], ALU.add).then_inc(chosen_ready, 1)
                dve.wait_ge(ex_ready, j + 1)
                rstep(dve.tensor_scalar_add(exp1[:, qs], ex[:, qs], 1.0))
                after()
                rstep(dve.reciprocal(gates[:, 0, qs], exp1[:, qs]))
                after()
                rstep(dve.tensor_tensor(gates[:, 1, qs], ex[:, qs], gates[:, 0, qs], ALU.mult))
                after()
                dve.tensor_copy(rows_sb[:, :, bass.ds(first, tiles), D], gates[:, :, qs]).then_inc(gates_set, 1)
                dve.wait_ge(rank_done, j + 1)
                ranks = rank_ps[:, 0:tiles * E].rearrange("p (q e) -> p q e", e=E)
                counted = rstep(dve.tensor_tensor(count_n[:, :], rank_ps[:, tiles * E:(tiles + 1) * E], count[:, :], ALU.add))
                rstep(dve.tensor_tensor(slot_a[:, qs, :], ranks, bc(left, tiles), ALU.is_ge))
                after(counted)
                padded = rstep(dve.tensor_scalar_add(room_i[:, 0, :], count_n[:, :], float(P - 1)))
                rstep(dve.tensor_tensor(slot_c[:, qs, :], ranks, bc(base, tiles), ALU.add))
                after(padded)
                rstep(dve.tensor_scalar(room_i[:, 1, :], room_i[:, 0, :], -P, None, ALU.bitwise_and))
                after()
                rstep(dve.tensor_copy(room_n[:, :], room_i[:, 1, :]))
                after()
                rstep(dve.tensor_tensor(added[:, :], room_n[:, :], room[:, :], ALU.subtract))
                after()
                rstep(dve.tensor_tensor_scan(ends[:, :], added[:, :], zero_e[:, :], given[:, 0:1], ALU.add, ALU.add))
                after()
                rstep(dve.tensor_tensor(shift_n[:, :], ends[:, :], room_n[:, :], ALU.subtract))
                after()
                rstep(dve.tensor_tensor(shift_d[:, :], shift_n[:, :], shift[:, :], ALU.subtract))
                after()
                rstep(dve.tensor_tensor(slot_b[:, qs, :], slot_a[:, qs, :], bc(shift_d, tiles), ALU.mult))
                after()
                rstep(dve.tensor_tensor(slot[:, qs, :], slot_c[:, qs, :], slot_b[:, qs, :], ALU.add))
                after()
                for k in range(K):
                    last = dve.tensor_tensor(weighted[:, k, qs, :], onehot[:, k, qs, :], slot[:, qs, :], ALU.mult)
                rstep(last)
                after()
                rstep(dve.reduce_sum(slot_k[:, :, qs], weighted[:, :, qs, :], axis=AX.X))
                after()
                dve.tensor_copy(slot_of[:, :, bass.ds(first, tiles)], slot_k[:, :, qs]).then_inc(slots_ready, 1)
                for k in range(K):
                    last = dve.tensor_tensor(weighted[:, k, qs, :], onehot[:, k, qs, :], by_tile(gates[:, k, qs], tiles), ALU.mult)
                rstep(last)
                rstep(dve.tensor_copy(count[:, :], count_n[:, :]))
                rstep(dve.tensor_copy(room[:, :], room_n[:, :]))
                rstep(dve.tensor_copy(given[:, :], ends[:, E - 1:E]))
                rstep(dve.tensor_tensor(left[:, :], room_n[:, :], count_n[:, :], ALU.subtract))
                rstep(dve.scalar_tensor_tensor(opened[:, :], added[:, :], 0.0, shift_d[:, :], ALU.is_gt, ALU.mult))
                after()
                rstep(dve.tensor_tensor(shift_n[:, :], opened[:, :], shift[:, :], ALU.add))
                rstep(dve.tensor_scalar(le[:, :], ends[:, :], block_start, 0.0, ALU.is_le, ALU.add, accum_out=le_n[:, :]))
                after()
                rstep(dve.tensor_copy(shift[:, :], shift_n[:, :]))
                rstep(dve.tensor_tensor(base[:, :], shift_n[:, :], count_n[:, :], ALU.add))
                rstep(dve.scalar_tensor_tensor(le_m[:, :], le_n[:, :], float(E), le_n[:, :], ALU.is_lt, ALU.mult))
                dve.tensor_tensor(combine[:, bass.ds(first, tiles), :], weighted[:, 0, qs, :], weighted[:, 1, qs, :],
                                  ALU.add).then_inc(combine_ready, 1)
                after()
                rstep(dve.tensor_tensor(expert_of[:, :], expert_of[:, :], le_m[:, :], ALU.add))
                after()
                assert done[0] == R_STEPS, done[0]

            with dve.Fori(0, WHOLE) as j:
                route_chunk(j, TPC * j, TPC)
            def add_bias(c, half, source):
                x1 = x_sb[:, bass.ds(c * TPC + half * TAIL, TAIL), :]
                dve.tensor_tensor(x1, source[:, half * TAIL * D:(half + 1) * TAIL * D].rearrange("p (q d) -> p q d", d=D), x1,
                                  ALU.add).then_inc(bias_added, 1)

            dve.wait_ge(experts_turned, 1)
            dve.tensor_copy(expert_row[0:1, 0:TURN], expert_ps[0:1, 0:TURN]).then_inc(experts_known, 1)
            for c in range(2):
                route_chunk(WHOLE + c, TPC * WHOLE + TAIL * c, TAIL)
            dve.wait_ge(experts_turned, 2)
            dve.tensor_copy(expert_row[0:1, TURN:BLOCKS], expert_ps[0:1, TURN:BLOCKS]).then_inc(experts_known, 1)
            for c in range(2 * PAIRS):
                for half in range(2):
                    dve.wait_ge(bias_done, c // 2 + 1)
                    add_bias(c, half, bias_banks[c % 2])
            dve.wait_ge(combine_ready, CHUNKS)

            def copy_t(n, m):
                dve.wait_ge(xbt_done, n + 1)
                if not isinstance(n, int) or n >= 2:
                    dve.wait_ge(hid_done, n - 1)
                dve.tensor_copy(xb_t[:, m % 2, :], bank[m % 2][:, 0:P]).then_inc(xbt_copied, 1)

            def scale_turn(i, last):
                for m in range(TURN):
                    n = TURN * i + m
                    if not last or m + 2 < TURN:
                        copy_t(n + 2, m)
                    if isinstance(n, int) and n in SUM_AFTER:
                        finish_part(*SUM_AFTER[n])
                    if m == BIAS_AT[0]:
                        dve.wait_ge(combt_done, PAIRS + i)
                        dve.tensor_copy(staged[:, :, :],
                                        combine[:, bass.ds((2 * PAIRS + i) * TPC, TPC), :]).then_inc(gates_staged, 1)
                    if m in (BIAS_AT[4], BIAS_AT[4] + 1):
                        dve.wait_ge(bias_done, PAIRS + i + 1)
                        add_bias(2 * PAIRS + i, m - BIAS_AT[4], bias_banks[0])
                    y = m % YRING
                    ring = RINGS * i + m // YRING
                    if m % QUAD == 0:
                        dve.wait_ge(xb_in[y // QUAD], 16 * (ring + 1))
                        if not isinstance(ring, int) or ring >= 1:
                            for u in range(QUAD):
                                dve.wait_ge(y_out[y + u], 16 * ring)
                        dve.tensor_scalar(y_to[:, y:y + QUAD], xb[:, y // QUAD, :, D + 1], -1.0, float(K * N), ALU.mult, ALU.add)
                    dve.wait_ge(y_done, n + 1)
                    dve.tensor_scalar(y_sb[:, y, :], bank[4 + m % 2][:, 0:D], xb[:, y // QUAD, y % QUAD, D:D + 1], None,
                                      ALU.mult).then_inc(y_ready, 1)
                    if m % QUAD == QUAD - 1:
                        dve.engine_nop().then_inc(xb_free, 1)

            def finish_part(c, part):
                k, half = part // 2, part % 2
                ts = slice(c * TPC + half * TAIL, c * TPC + (half + 1) * TAIL)
                if part == 0:
                    dve.wait_ge(pairs_in[c], 16 * K)
                    dve.wait_ge(bias_added, 2 * (c + 1))
                if k == 1:
                    dve.wait_ge(f_step, SUM_PARTS * c + half + 1)
                dve.tensor_tensor(x_sb[:, ts, :], x_sb[:, ts, :], pairs_sb[:, k, ts, :], ALU.add).then_inc(f_step, 1)

            copy_t(0, 0)
            copy_t(1, 1)
            scale_turn(0, False)
            with dve.Fori(1, TURNS - 1) as i:
                scale_turn(i, False)
            scale_turn(TURNS - 1, True)
            for c in range(len(SUM_AFTER) // SUM_PARTS, OUTS):
                for part in range(SUM_PARTS):
                    finish_part(c, part)

        @block.tensor
        def _(pe):
            def accumulate(s, bank_acc):
                for i in range(CPS):
                    c = s * CPS + i
                    last = pe.matmul(bank_acc[:, :], h_sb[:, c, :], adj_sb[:, s, i, :], start=(c == 0), stop=(c == TILES - 1))
                last.then_inc(adj_used, 1)

            pe.wait_ge(consts_in, 16)
            for c in range(TILES + G_LAG):
                if c == 0:
                    pe.wait_ge(gnn_w_in, 32)
                if 2 <= c < TILES + 2:
                    t = c - 2
                    pe.wait_ge(xnt_copied, t + 1)
                    if t % GROUP == 0 and t >= 2 * GROUP:
                        pe.wait_ge(h_ready, t // GROUP - 1)
                    pe.matmul(h_ps[t // GROUP % 2][:, t % GROUP * D:(t % GROUP + 1) * D], xn_t[:, t % 2, :], wt[:, :],
                              start=True, stop=True).then_inc(h_done, 1)
                if c >= G_LAG:
                    t = c - G_LAG
                    pe.wait_ge(h_ready, t // GROUP + 1)
                    if t % CPS == 0:
                        pe.wait_ge(adj_in[t // CPS], 16)
                    last = pe.matmul(acc[0][:, :], h_sb[:, t, :], adj_sb[:, t // CPS, t % CPS, :], start=(t == 0), stop=(t == TILES - 1))
                    if t % CPS == CPS - 1:
                        last.then_inc(adj_used, 1)
                if c < TILES:
                    pe.wait_ge(xn_ready, c + 1)
                    pe.transpose(bank[c % 2][:, 0:P], h_sb[:, c, :], ident).then_inc(xnt_done, 1)

            def back(j, tiles):
                pe.wait_ge(agg_copied, j + 1)
                for q in range(tiles):
                    last = pe.transpose(agg_ps[:, q * P:(q + 1) * P], agg_t[:, q * P:(q + 1) * P], ident)
                last.then_inc(agg_back, 1)

            def turn_rows(j, tiles):
                pe.wait_ge(xln_ready, j + 1)
                for q in range(tiles):
                    last = pe.transpose(xlnt_ps[:, q * P:(q + 1) * P], xln[:, q, :], ident)
                last.then_inc(xlnt_done, 1)

            def route(j, tiles):
                pe.wait_ge(xlnt_copied, j + 1)
                for q in range(tiles):
                    last = pe.matmul(logit_ps[:, q * E:(q + 1) * E], xln_t[:, q * P:(q + 1) * P], wr[:, :], start=True, stop=True)
                last.then_inc(logits_done, 1)

            def count_ranks(j, tiles):
                pe.wait_ge(chosen_ready, j + 1)
                for q in range(tiles + 1):
                    for r in range(min(q + 1, tiles)):
                        last = pe.matmul(rank_ps[:, q * E:(q + 1) * E], (tri if r == q else ones)[:, :], chosen[:, r, :],
                                         start=(r == 0), stop=(r == min(q, tiles - 1)))
                last.then_inc(rank_done, 1)

            def bias_product(target, at, h):
                return pe.matmul(target[:, 2 * at * D:2 * (at + 1) * D], combine_t[:, h * P:(h + 1) * P],
                                 b2_sb[:, :, :].rearrange("p h d -> p (h d)"), start=True, stop=True)

            def bias_pair(p):
                pe.wait_ge(combine_ready, 2 * (p + 1))
                for h in range(TPC):
                    t = 2 * (p * TPC + h)
                    last = pe.transpose(combt_ps[:, h * P:(h + 1) * P], combine[:, t:t + 2, :].rearrange("p q e -> p (q e)"), ident)
                last.then_inc(combt_done, 1)
                pe.wait_ge(combt_copied, p + 1)
                if p >= 1:
                    pe.wait_ge(bias_added, 4 * p)
                for h in range(TPC):
                    last = bias_product(bias_banks[h // 2], h % 2, h)
                last.then_inc(bias_done, 1)

            def turn_experts(chunks):
                pe.wait_ge(r_step, R_STEPS * chunks)
                if chunks == CHUNKS:
                    pe.wait_ge(experts_known, 1)
                pe.matmul(expert_ps[0:1, 0:BLOCKS], expert_of[:, 0:1], ident, start=True, stop=True).then_inc(experts_turned, 1)

            def chunk(j, par):
                for s in range(SLOTS):
                    pe.wait_ge(adj_in[s], 16 * (j + 1))
                    accumulate(s, acc[par])
                    if s in (0, 2, 3, 5):
                        {0: back, 2: turn_rows, 3: route, 5: count_ranks}[s](j - 1, TPC)

            EXPERTS_AT = 9

            def tail_chunk(c, tiles_before, places):
                j = WHOLE + c
                for t in range(TILES):
                    s = c * SLOTS // 2 + t // (2 * CPS)
                    if t % (2 * CPS) == 0:
                        pe.wait_ge(adj_in[s], 16 * (WHOLE + 1))
                    last = pe.matmul(acc[j % 2][:, 0:TAIL * P], h_sb[:, t, :], tail_sb[:, s, t % (2 * CPS), :],
                                     start=(t == 0), stop=(t == TILES - 1))
                    if t % (2 * CPS) == 2 * CPS - 1:
                        last.then_inc(adj_used, 1)
                    if t in places:
                        (back, turn_rows, route, count_ranks)[places.index(t)](j - 1, tiles_before)
                    if c == 1 and t == EXPERTS_AT:
                        turn_experts(WHOLE)

            pe.wait_ge(router_w_in, 4 * 16)
            pe.wait_ge(small_ready, 2)
            with pe.Fori(0, (WHOLE - 1) // 2) as jj:
                chunk(2 * jj + 1, 1)
                chunk(2 * jj + 2, 0)
            tail_chunk(0, TPC, (2, 11, 13, 21))
            tail_chunk(1, TAIL, (2, 13, 15, 21))
            for piece in (back, turn_rows, route, count_ranks):
                piece(CHUNKS - 1, TAIL)
            bias_pair(0)
            turn_experts(CHUNKS)
            bias_pair(1)

            def turn_block(i, m):
                n = TURN * i + m
                q = m % YRING // QUAD
                if m % QUAD == 0:
                    pe.wait_ge(xb_in[q], 16 * (RINGS * i + m // YRING + 1))
                pe.transpose(bank[m % 2][:, 0:P], xb[:, q, m % QUAD, 0:D], ident).then_inc(xbt_done, 1)

            def first_layer(i, m):
                n = TURN * i + m
                pe.wait_ge(wb_in[m], 16 * (i + 1))
                pe.wait_ge(xbt_copied, n + 1)
                for f in range(HID // P):
                    last = pe.matmul(bank[2 + m % 2][:, f * P:(f + 1) * P], weights(m, f * P, (f + 1) * P), xb_t[:, m % 2, :],
                                     start=True, stop=True)
                last.then_inc(hid_done, 1)

            def second_layer(i, m):
                n = TURN * i + m
                pe.wait_ge(hid_ready, n + 1)
                if not isinstance(n, int) or n >= 2:
                    pe.wait_ge(y_ready, n - 1)
                for f in range(HID // P):
                    last = pe.matmul(bank[4 + m % 2][:, 0:D], hid_t[:, m % 2, f, :], weights(m, HID + f * D, HID + (f + 1) * D),
                                     start=(f == 0), stop=(f == HID // P - 1))
                last.then_inc(y_done, 1)

            def turn_gates(i):
                pe.wait_ge(gates_staged, i + 1)
                for h in range(TPC // 2):
                    last = pe.transpose(combt_ps[:, h * P:(h + 1) * P], staged[:, 2 * h:2 * h + 2, :].rearrange("p q e -> p (q e)"),
                                        ident)
                last.then_inc(combt_done, 1)

            def second_bias(i):
                pe.wait_ge(combt_copied, PAIRS + i + 1)
                pe.wait_ge(bias_added, 2 * (2 * PAIRS + i))
                for h in range(TPC // 2):
                    last = bias_product(bias_banks[0], h, h)
                last.then_inc(bias_done, 1)

            def expert_turn(i, last):
                for m in range(TURN):
                    if m == BIAS_AT[1]:
                        turn_gates(i)
                    if m == BIAS_AT[3]:
                        second_bias(i)
                    if not last or m + 2 < TURN:
                        turn_block(i + (m + 2) // TURN, (m + 2) % TURN)
                    if not last or m + 1 < TURN:
                        first_layer(i + (m + 1) // TURN, (m + 1) % TURN)
                    second_layer(i, m)

            pe.wait_ge(experts_known, 2)
            turn_block(0, 0)
            turn_block(0, 1)
            first_layer(0, 0)
            expert_turn(0, False)
            with pe.Fori(1, TURNS - 1) as i:
                expert_turn(i, False)
            expert_turn(TURNS - 1, True)


def kernel(x, adj, L0_gnn_W, L0_gnn_b, L0_ffn_Wr, L0_ffn_br, L0_ffn_W1, L0_ffn_b1, L0_ffn_W2, L0_ffn_b2):
    import numpy as np
    import concourse.bacc as bacc
    from concourse.bass_utils import run_bass_kernel_spmd

    adj = np.asarray(adj)
    adj_t = adj[:WHOLE * CHUNK].reshape(WHOLE, CHUNK, TILES, P).transpose(0, 3, 2, 1)
    adj_tail = adj[WHOLE * CHUNK:].reshape(2, TAIL * P, TILES, P).transpose(0, 3, 2, 1)
    w1 = np.asarray(L0_ffn_W1)
    w2 = np.asarray(L0_ffn_W2).reshape(E, HID // P, P, D).transpose(0, 2, 1, 3).reshape(E, P, HID // P * D)
    b1 = np.asarray(L0_ffn_b1).reshape(E, HID // P, P).transpose(0, 2, 1)
    consts = np.zeros((P, C_COLS), np.float32)
    consts[:, C_ID:C_ID + P] = np.eye(P)
    consts[:, C_TRI:C_TRI + P] = np.triu(np.ones((P, P)), 1)
    consts[:, C_IOTA:C_IOTA + E] = np.arange(E)
    consts[:, C_DEST:C_BLK] = K * N - (np.arange(K * TILES)[None, :] * P + np.arange(P)[:, None])
    consts[:, C_BLK] = np.arange(P) * P
    ins = {
        "x": x, "adj_t": adj_t, "adj_tail": adj_tail, "w_t": np.asarray(L0_gnn_W).T, "b": L0_gnn_b, "w_router": L0_ffn_Wr,
        "b_router": L0_ffn_br, "w_experts": np.concatenate([w1, w2, b1], axis=2), "b2": L0_ffn_b2, "consts": consts,
    }
    ins = {name: np.ascontiguousarray(a) for name, a in ins.items()}
    nc = bacc.Bacc("TRN2", target_bir_lowering=False, num_devices=1)
    F32 = mybir.dt.float32
    args = {name: nc.dram_tensor(name, a.shape, F32, kind="ExternalInput").ap() for name, a in ins.items()}
    out = nc.dram_tensor("out", [N, D], F32, kind="ExternalOutput").ap()
    gnn_moe(nc, **args, out=out)
    r = run_bass_kernel_spmd(nc, [ins], core_ids=[0])
    return r.results[0]["out"]
```
